# Optimizing a Trainium2 kernel written in Bass

```python
import numpy as np
import jax
import jax.numpy as jnp

def _softmax(x, axis=-1):
    return jax.nn.softmax(x, axis=axis)

def _gelu(x):
    return jax.nn.gelu(x, approximate=True)

def _silu(x):
    return jax.nn.silu(x)

def _sigmoid(x):
    return jax.nn.sigmoid(x)

def _layernorm(x, axis=-1, eps=1e-05):
    m = jnp.mean(x, axis=axis, keepdims=True)
    v = jnp.var(x, axis=axis, keepdims=True)
    return (x - m) / jnp.sqrt(v + eps)

def _scatter_add(tgt, idx, src, axis=0):
    return tgt.at[idx].add(src)

def _segment_sum(src, seg, n):
    return jax.ops.segment_sum(src, seg, n)
kernel_name = 'mk_seq_preln_d1_jaxref_r8_b1a0a3'

def setup_inputs(seed: int=0):
    np.random.seed(seed)
    _w = jnp.asarray

    def _L0_attn_setup():
        import jax, jax.numpy as jnp
        import numpy as np
        N_EMBD = 128
        N_HEAD = 16
        HEAD_DIM = N_EMBD // N_HEAD
        KV_RANK = 32
        Q_RANK = 64
        ROPE_DIM = 32
        B, T = (2, 256)
        EPS = 1e-06

        def _rope_tables(T, dim):
            inv_freq = 1.0 / 10000.0 ** (np.arange(0, dim, 2, dtype=np.float32) / dim)
            t = np.arange(T, dtype=np.float32)
            freqs = np.outer(t, inv_freq)
            emb = np.concatenate([freqs, freqs], -1)
            return (jnp.asarray(np.cos(emb)), jnp.asarray(np.sin(emb)))

        def _apply_rope(x, cos, sin):
            d2 = x.shape[-1] // 2
            x1, x2 = (x[..., :d2], x[..., d2:])
            rot = jnp.concatenate([-x2, x1], axis=-1)
            return x * cos[None, None, :, :] + rot * sin[None, None, :, :]
        key = jax.random.key(seed)
        ks = jax.random.split(key, 10)

        def w(k, fan_in, fan_out):
            return jax.random.normal(k, (fan_in, fan_out), dtype=jnp.float32) * fan_in ** (-0.5)
        return {'x': jax.random.normal(ks[0], (B, T, N_EMBD), dtype=jnp.float32), 'W_kv': w(ks[1], N_EMBD, KV_RANK), 'g_kv': jnp.ones((KV_RANK,), dtype=jnp.float32), 'W_kdec': w(ks[2], KV_RANK, N_HEAD * HEAD_DIM), 'W_vdec': w(ks[3], KV_RANK, N_HEAD * HEAD_DIM), 'W_q': w(ks[4], N_EMBD, Q_RANK), 'W_qdec': w(ks[5], Q_RANK, N_HEAD * HEAD_DIM), 'W_krope': w(ks[6], N_EMBD, N_HEAD * ROPE_DIM), 'W_qrope': w(ks[7], Q_RANK, N_HEAD * ROPE_DIM), 'W_o': w(ks[8], N_HEAD * HEAD_DIM, N_EMBD)}
    _L0_attn_in = _L0_attn_setup()

    def _L0_ffn_setup():
        import jax, jax.numpy as jnp
        import numpy as np
        H = 128
        I = 352
        E = 8
        TOP_K = 2

        def _moe(hidden_states, router_w, gate_w, up_w, down_w):
            B, S, Hd = hidden_states.shape
            x = hidden_states.reshape(-1, Hd)
            logits = x @ router_w.T
            probs = jax.nn.softmax(logits.astype(jnp.float32), axis=-1)
            top_w, top_idx = jax.lax.top_k(probs, TOP_K)
            top_w = top_w.astype(x.dtype)
            onehot = jax.nn.one_hot(top_idx, E, dtype=x.dtype)
            w_te = jnp.einsum('tk,tke->te', top_w, onehot)
            g = jnp.einsum('th,eih->tei', x, gate_w)
            u = jnp.einsum('th,eih->tei', x, up_w)
            h = jax.nn.silu(g) * u
            y = jnp.einsum('tei,ehi,te->th', h, down_w, w_te)
            return y.reshape(B, S, Hd)
        key = jax.random.key(seed)
        ks = jax.random.split(key, 5)
        s = 0.02
        return {'hidden_states': jax.random.normal(ks[0], (2, 128, H), dtype=jnp.float32), 'router_w': jax.random.normal(ks[1], (E, H), dtype=jnp.float32) * s, 'gate_w': jax.random.normal(ks[2], (E, I, H), dtype=jnp.float32) * s, 'up_w': jax.random.normal(ks[3], (E, I, H), dtype=jnp.float32) * s, 'down_w': jax.random.normal(ks[4], (E, H, I), dtype=jnp.float32) * s}
    _L0_ffn_in = _L0_ffn_setup()
    _d = {'L0_attn_x': _L0_attn_in['x'], 'L0_attn_W_kv': _L0_attn_in['W_kv'], 'L0_attn_g_kv': _L0_attn_in['g_kv'], 'L0_attn_W_kdec': _L0_attn_in['W_kdec'], 'L0_attn_W_vdec': _L0_attn_in['W_vdec'], 'L0_attn_W_q': _L0_attn_in['W_q'], 'L0_attn_W_qdec': _L0_attn_in['W_qdec'], 'L0_attn_W_krope': _L0_attn_in['W_krope'], 'L0_attn_W_qrope': _L0_attn_in['W_qrope'], 'L0_attn_W_o': _L0_attn_in['W_o'], 'L0_ffn_router_w': _L0_ffn_in['router_w'], 'L0_ffn_gate_w': _L0_ffn_in['gate_w'], 'L0_ffn_up_w': _L0_ffn_in['up_w'], 'L0_ffn_down_w': _L0_ffn_in['down_w']}
    _x0 = _d['L0_attn_x']
    _d['L0_attn_x'] = jax.random.normal(jax.random.fold_in(jax.random.key(seed), 1), (2, 1024, 128), dtype=_x0.dtype)
    del _x0
    return _d

def reference(L0_attn_x, L0_attn_W_kv, L0_attn_g_kv, L0_attn_W_kdec, L0_attn_W_vdec, L0_attn_W_q, L0_attn_W_qdec, L0_attn_W_krope, L0_attn_W_qrope, L0_attn_W_o, L0_ffn_router_w, L0_ffn_gate_w, L0_ffn_up_w, L0_ffn_down_w):

    def _L0_attn_ref(x, W_kv, g_kv, W_kdec, W_vdec, W_q, W_qdec, W_krope, W_qrope, W_o):
        import jax, jax.numpy as jnp
        import numpy as np
        N_EMBD = 128
        N_HEAD = 16
        HEAD_DIM = N_EMBD // N_HEAD
        KV_RANK = 32
        Q_RANK = 64
        ROPE_DIM = 32
        B, T = (2, 256)
        EPS = 1e-06

        def _rope_tables(T, dim):
            inv_freq = 1.0 / 10000.0 ** (np.arange(0, dim, 2, dtype=np.float32) / dim)
            t = np.arange(T, dtype=np.float32)
            freqs = np.outer(t, inv_freq)
            emb = np.concatenate([freqs, freqs], -1)
            return (jnp.asarray(np.cos(emb)), jnp.asarray(np.sin(emb)))

        def _apply_rope(x, cos, sin):
            d2 = x.shape[-1] // 2
            x1, x2 = (x[..., :d2], x[..., d2:])
            rot = jnp.concatenate([-x2, x1], axis=-1)
            return x * cos[None, None, :, :] + rot * sin[None, None, :, :]
        Bx, Tx, C = x.shape
        kv_c = x @ W_kv
        kv_c = kv_c * jax.lax.rsqrt(jnp.mean(kv_c * kv_c, axis=-1, keepdims=True) + EPS) * g_kv
        q_c = x @ W_q

        def heads(y, d):
            return y.reshape(Bx, Tx, N_HEAD, d).transpose(0, 2, 1, 3)
        k_content = heads(kv_c @ W_kdec, HEAD_DIM)
        v = heads(kv_c @ W_vdec, HEAD_DIM)
        q_content = heads(q_c @ W_qdec, HEAD_DIM)
        k_rope = heads(x @ W_krope, ROPE_DIM)
        q_rope = heads(q_c @ W_qrope, ROPE_DIM)
        cos, sin = _rope_tables(Tx, ROPE_DIM)
        q_rope = _apply_rope(q_rope, cos, sin)
        k_rope = _apply_rope(k_rope, cos, sin)
        q = jnp.concatenate([q_content, q_rope], axis=-1)
        k = jnp.concatenate([k_content, k_rope], axis=-1)
        scale = 1.0 / jnp.sqrt(jnp.float32(q.shape[-1]))
        scores = jnp.einsum('bhqd,bhkd->bhqk', q, k) * scale
        causal = jnp.tril(jnp.ones((Tx, Tx), dtype=bool))
        scores = jnp.where(causal[None, None], scores, jnp.float32(-jnp.inf))
        attn = jax.nn.softmax(scores, axis=-1)
        out = jnp.einsum('bhqk,bhkd->bhqd', attn, v)
        out = out.transpose(0, 2, 1, 3).reshape(Bx, Tx, N_HEAD * HEAD_DIM)
        return out @ W_o

    def _L0_ffn_ref(hidden_states, router_w, gate_w, up_w, down_w):
        import jax, jax.numpy as jnp
        import numpy as np
        H = 128
        I = 352
        E = 8
        TOP_K = 2

        def _moe(hidden_states, router_w, gate_w, up_w, down_w):
            B, S, Hd = hidden_states.shape
            x = hidden_states.reshape(-1, Hd)
            logits = x @ router_w.T
            probs = jax.nn.softmax(logits.astype(jnp.float32), axis=-1)
            top_w, top_idx = jax.lax.top_k(probs, TOP_K)
            top_w = top_w.astype(x.dtype)
            onehot = jax.nn.one_hot(top_idx, E, dtype=x.dtype)
            w_te = jnp.einsum('tk,tke->te', top_w, onehot)
            g = jnp.einsum('th,eih->tei', x, gate_w)
            u = jnp.einsum('th,eih->tei', x, up_w)
            h = jax.nn.silu(g) * u
            y = jnp.einsum('tei,ehi,te->th', h, down_w, w_te)
            return y.reshape(B, S, Hd)
        return _moe(hidden_states, router_w, gate_w, up_w, down_w)
    x = L0_attn_x
    x = x + _L0_attn_ref(_layernorm(x, axis=-1), L0_attn_W_kv, L0_attn_g_kv, L0_attn_W_kdec, L0_attn_W_vdec, L0_attn_W_q, L0_attn_W_qdec, L0_attn_W_krope, L0_attn_W_qrope, L0_attn_W_o)
    x = x + _L0_ffn_ref(_layernorm(x, axis=-1), L0_ffn_router_w, L0_ffn_gate_w, L0_ffn_up_w, L0_ffn_down_w)
    return x

_drawn_inputs = setup_inputs


def setup_inputs(seed=0):
    import zlib

    import numpy as np

    out = dict(_drawn_inputs(seed))
    spreads = {'L0_attn_g_kv': (1.0, 0.2)}
    factors = {'L0_ffn_router_w': 8.0, 'L0_ffn_gate_w': 8.0, 'L0_ffn_up_w': 8.0, 'L0_ffn_down_w': 8.0}
    for name, (base, spread) in spreads.items():
        noise = np.random.default_rng([zlib.crc32(name.encode()), seed]).standard_normal(out[name].shape)
        drawn = base * np.exp(spread * noise) if base else spread * noise
        out[name] = jnp.asarray(drawn.astype(out[name].dtype))
    for name, factor in factors.items():
        out[name] = (out[name] * factor).astype(out[name].dtype)
    return out
```

```python
from contextlib import ExitStack

import numpy as np

import concourse.bass as bass
from concourse import mybir

F32 = mybir.dt.float32
F32R = mybir.dt.float32r
ALU = mybir.AluOpType
ACT = mybir.ActivationFunctionType

P = 128
B, T, D = 2, 1024, 128
NT = B * T // P
H, DH, R = 16, 8, 32
RKV, RQ = 32, 64
HG = 4
G = H // HG
UNITS = B * G
CH = 512
NC = T // CH
KT = CH // P
VW = DH + 1
QK = 3 * (R + DH)
SCALE = float(1.0 / np.sqrt(np.float32(DH + R)))
NEG = -3.0e38

DIAG = [CH - P * d for d in range(KT)]
PCOLS = [c * KT * CH + sum(DIAG) for c in range(NC)]


def p_off(c, kt):
    return kt * CH if kt < c * KT else c * KT * CH + sum(DIAG[:kt - c * KT])


WORK = [KT, 2 * KT]


def before(c, j):
    return c * HG * WORK[0] + j * WORK[c]


PER_UNIT = HG * sum(WORK)
ITEMS = NC * HG
SLOTS = PER_UNIT // ITEMS
LEAD = 2 * SLOTS
SCORES = [[(0,), (1,), (), (2,), (3,), ()], [(0, 1), (2,), (3,), (4, 5), (6,), (7,)]]


def chunk_of(n):
    for m in range(ITEMS):
        c, j = m // HG, m % HG
        if n < before(c, j) + WORK[c]:
            return m, n - before(c, j)


def plan(s, k):
    n = LEAD + SLOTS * s + k
    nxt, n = n >= PER_UNIT, n % PER_UNIT
    last = n - 2 if n >= 2 else n - 2 + PER_UNIT
    m, i = chunk_of(last)
    turned = m if i == WORK[m // HG] - 1 else None
    return nxt, n, turned, nxt and n >= 2


PRODUCTS = {(q // 2, 3 * (q % 2)): q for q in range(8)}
QUADS = sum(WORK)

E, I = 8, 352
IT = [P, P, I - 2 * P]
GU = 2 * I
WC = GU + len(IT) * D
NB = B * T // CH



def attention(nc, x, w_qkv, w_kdec, w_vdec, w_qdec, g_kv, w_kr, w_qr, cosT, sinT, attn):
    con = nc.dram_tensor("content", (6, DH * H, B * T), F32, kind="Internal").ap()
    with ExitStack() as ctx:
        def sb(name, shape, dt=F32):
            return ctx.enter_context(nc.sbuf_tensor(name, shape, dt))

        def sem(name):
            return ctx.enter_context(nc.semaphore(name))

        xnT = sb("xnT", [P, B * T])
        qcT = sb("qcT", [RQ, B * T])
        vals = sb("vals", [P, NT, H, VW])
        vals0 = sb("vals0", [P, KT, HG, VW])
        vals1 = sb("vals1", [P, 2 * KT, HG, VW])
        att = sb("att", [P, NC, KT, HG * DH])
        cos = sb("cos", [P, T])
        sin = sb("sin", [P, T])
        mask = sb("mask", [P, CH])
        ident = sb("ident", [P, P])
        gkv = sb("gkv", [P, 1])
        wkr = sb("wkr", [P, 2, P])
        wqr = sb("wqr", [RQ, 2, P])
        qs = [sb(f"qs{p}", [P, HG, T], F32R) for p in range(2)]
        ks = [sb(f"ks{p}", [P, HG, T], F32R) for p in range(2)]
        rot = [[sb(f"rot_{a}{p}", [P, T], F32R) for p in "hl"] for a in "kq"]
        t1 = sb("t1", [P, 3, CH])
        t2 = sb("t2", [P, 2, CH])
        m4 = sb("m4", [P, HG, KT])
        mrow = sb("mrow", [KT, 2, P], F32R)
        oT = sb("oT", [P, 2, CH])
        rec = sb("rec", [P, KT, HG])
        probs = [sb(f"probs{c}", [P, HG, PCOLS[c]]) for c in range(NC)]
        rstd = sb("rstd", [P, NT])
        krs = sb("krs", [P, NT])
        eps = sb("eps", [P, 2])

        bank = [ctx.enter_context(nc.psum_tensor(f"bank{i}", [P, CH], F32)) for i in range(8)]
        MX, ST = bank[0:2], bank[2:5]
        PV, MT, WK = bank[5], bank[6], bank[7]

        ld_x = [sem(f"ld_x{i}") for i in range(4)]
        ld_w = sem("ld_w")
        ld_tab = sem("ld_tab")
        consts = sem("consts")
        gscaled = sem("gscaled")
        bnd = sem("bnd")
        mvd = sem("mvd")
        rsd = sem("rsd")
        rrd = sem("rrd")
        rbd = sem("rbd")
        xnd = sem("xnd")
        tpd = sem("tpd")
        xnTd = sem("xnTd")
        qkvd = sem("qkvd")
        kvcd = sem("kvcd")
        qcd = sem("qcd")
        msd = sem("msd")
        krd = sem("krd")
        kr_in = sem("kr_in")
        kvnd = sem("kvnd")
        cond = sem("cond")
        conh = sem("conh")
        conl = sem("conl")
        vpd = sem("vpd")
        vsd = sem("vsd")
        con_st = [sem(f"con_st_{a}") for a in "kq"]
        ks_ones = sem("ks_ones")
        ld_wr = sem("ld_wr")
        wk_full = sem("wk_full")
        wk_free = sem("wk_free")
        s_ready = sem("s_ready")
        h_ready = sem("h_ready")
        l_ready = sem("l_ready")
        ld_con = [sem(f"ld_con{p}") for p in range(2)]
        ld_stk = [[sem(f"ld_stk{p}{j}") for j in range(HG)] for p in range(2)]
        att_st = [sem(f"att_st{c}") for c in range(NC)]
        att_ok = sem("att_ok")
        ld_m = [sem(f"ld_m{j}") for j in range(HG)]
        mx_done = sem("mx_done")
        mx_read = sem("mx_read")
        mt_done = sem("mt_done")
        mrow_ok = sem("mrow_ok")
        st_done = sem("st_done")
        exp_done = sem("exp_done")
        masked = sem("masked")
        pv_done = sem("pv_done")
        pv_read = sem("pv_read")
        v0_ok = sem("v0_ok")
        v1_ok = sem("v1_ok")
        rec_ok = sem("rec_ok")
        passed = {e.engine: sem(f"passed_{n}") for n, e in (("sp", nc.sync), ("pool", nc.gpsimd), ("dve", nc.vector))}

        block = ctx.enter_context(nc.Block())

        flat = probs[0][:, :, :].rearrange("p j c -> p (j c)")
        xs = flat[:, 0:NT * D].rearrange("p (t c) -> p t c", c=D)
        at = NT * D
        wqkv, wkd, wvd, wqd, ones = [flat[:, at + P * i:at + P * i + n]
                                     for i, n in enumerate((RQ + RKV, H * DH, H * DH, H * DH, RKV))]
        wqd = wqd[0:RQ, :]
        at += 5 * P
        stats = flat[:, at:at + 6 * NT].rearrange("p (t c) -> p t c", c=6)
        mv = flat[:, at + 6 * NT:at + 8 * NT].rearrange("p (t c) -> p t c", c=2)
        flat = probs[1][:, :, :].rearrange("p j c -> p (j c)")
        xn = flat[:, 0:4 * CH].rearrange("p (t c) -> p t c", c=D)
        kvc = flat[:, 4 * CH:8 * CH]
        kvq = flat[:, 8 * CH:12 * CH]
        krb = flat[:, 12 * CH:13 * CH]
        kvn = flat[:, 16 * CH:20 * CH]
        con_h = [flat[:, (20 + i) * CH:(21 + i) * CH] for i in range(2)]
        con_l = [flat[:, (22 + i) * CH:(23 + i) * CH] for i in range(2)]

        def wait(eng, s, v):
            if not isinstance(v, int) or v > 0:
                eng.wait_ge(s, v)

        def own(eng):
            eng.sem_inc(passed[eng.engine], 1)

        def unit_loop(eng, unit):
            unit(0, 0, 0, True, False)
            with eng.Fori(0, G - 1) as i:
                u = eng.snap(2 * i + 1)
                unit(u, 1, i, False, False)
                unit(u + 1, 0, i + 1, False, False)
            unit(UNITS - 1, 1, G - 1, False, True)

        def wk_before(u):
            return 10 * u + 6 if not isinstance(u, int) or u > 0 else 8

        def pv_before(u):
            return QUADS * u - 2 * KT if not isinstance(u, int) or u > 0 else 0

        @block.sync
        def _(sp):
            for c in range(NC):
                sp.sem_inc(att_st[c], 16)
            for i in range(4):
                sp.dma_start(xs[:, 4 * i:4 * i + 4, :], x[:, 4 * i:4 * i + 4, :]).then_inc(ld_x[i], 16)
            sp.dma_start(wqkv[:, :], w_qkv).then_inc(ld_w, 16)
            sp.dma_start(wkd[RQ:RQ + RKV, :], w_kdec).then_inc(ld_w, 16)
            sp.dma_start(wvd[RQ:RQ + RKV, :], w_vdec).then_inc(ld_w, 16)
            sp.dma_start(wqd[:, :], w_qdec).then_inc(ld_w, 16)
            sp.dma_start(gkv[RQ:RQ + RKV, :], g_kv).then_inc(ld_w, 16)
            sp.dma_start(cos[:, :], cosT).then_inc(ld_tab, 16)
            sp.dma_start(sin[:, :], sinT).then_inc(ld_tab, 16)

            def load_rot(g):
                sp.dma_start(wkr[:, :, :], w_kr[:, :, bass.ds(g * P, P)]).then_inc(ld_wr, 16)
                sp.dma_start(wqr[:, :, :], w_qr[:, :, bass.ds(g * P, P)]).then_inc(ld_wr, 16)

            load_rot(0)
            for i in range(4):
                for a in range(2):
                    n = 2 * i + a
                    sp.wait_ge(conl, n + 1)
                    for k, lo in enumerate(([0, 1, 0], [0, 0, 1])[a]):
                        sp.dma_start(con[3 * a + k, :, CH * i:CH * i + CH], (con_h, con_l)[lo][a])\
                          .then_inc(con_st[a], 16)
            def load_content(u, p, g):
                if not isinstance(u, int) or u > 1:
                    wait(sp, st_done, PER_UNIT * (u - 1))
                    own(sp)
                for a in range(2):
                    if isinstance(u, int) and u == 0:
                        sp.wait_ge(con_st[a], 16 * 12)
                    src = con[3 * a:3 * a + 3, :, T * p:T * p + T].rearrange("k (d h) t -> (k d) h t", h=H)
                    sp.dma_start((ks, qs)[a][p][3 * R:QK, :, :].bitcast(F32),
                                 src[:, bass.ds(g * HG, HG), :]).then_inc(ld_con[p], 16)

            def load_rotary(u, p, j, a):
                if j == 0:
                    own(sp)
                    wait(sp, l_ready, 4 * u + 2 * a + 2)
                for k, lo in enumerate(([0, 1, 0], [0, 0, 1])[a]):
                    sp.dma_start((ks, qs)[a][p][R * k:R * k + R, j, :].bitcast(F32),
                                 rot[a][lo][R * j:R * j + R, :].bitcast(F32)).then_inc(ld_stk[p][j], 16)

            def store_att(u, p, g, c):
                wait(sp, att_ok, 1 + 2 * u + c + 1)
                own(sp)
                sp.dma_start(attn[:, T // P * p + KT * c:T // P * p + KT * c + KT, bass.ds(g * (HG * DH), HG * DH)],
                             att[:, c, :, :]).then_inc(att_st[c], 16)

            load_content(0, 0, 0)
            for j in range(HG):
                for a in range(2):
                    load_rotary(0, 0, j, a)

            def unit(u, p, g, first, last):
                g1, gb = (g, g - 1) if p == 0 else (g + 1, g)
                for s in range(ITEMS):
                    if s == 2 and not last:
                        load_content(u + 1, 1 - p, g1)
                    if s == 4 and p == 0:
                        wait(sp, wk_full, wk_before(u) + 8)
                        own(sp)
                        load_rot((g + 1) % G)
                    for h in range(2):
                        n = 2 * s + h - 5
                        if 0 <= n < 2 * HG and not last:
                            wait(sp, st_done, PER_UNIT * u + before(s // HG, s % HG) + h * WORK[s // HG] // 2)
                            load_rotary(u + 1, 1 - p, n % HG, n // HG)
                    if s in (5, 7) and not first:
                        store_att(u - 1, 1 - p, gb, (s - 5) // 2)

            unit_loop(sp, unit)
            for c in range(NC):
                store_att(UNITS - 1, 1, G - 1, c)
                sp.wait_ge(att_st[c], 16 * (1 + UNITS))

        @block.gpsimd
        def _(pool):
            pool.memset(ident[:, :], 0.0).then_inc(consts, 1)
            pool.memset(mask[:, :], 0.0).then_inc(consts, 1)
            pool.wait_ge(consts, 2)
            pool.affine_select(out=ident[:, :], in_=ident[:, :], compare_op=ALU.not_equal, fill=1.0, base=0,
                               pattern=[[-1, P]], channel_multiplier=1).then_inc(consts, 1)
            pool.affine_select(out=mask[:, CH - P:CH], in_=mask[:, CH - P:CH], compare_op=ALU.is_ge, fill=NEG,
                               base=0, pattern=[[-1, P]], channel_multiplier=1).then_inc(consts, 1)
            pool.memset(ones[:, :], 1.0 / RKV).then_inc(consts, 1)
            pool.memset(eps[:, 0:1], 1e-5).then_inc(consts, 1)
            pool.memset(eps[:, 1:2], 1e-6).then_inc(consts, 1)
            pool.memset(vals[:, :, :, :], 1.0).then_inc(consts, 1)

            def rotary_sum(u, i):
                wait(pool, wk_free, 8 * u + 2 * i + 2)
                pool.tensor_tensor(out=t1[:, i % 3, :], in0=t1[:, i % 3, :], in1=t2[:, i % 2, :],
                                   op=ALU.add).then_inc(s_ready, 1)

            def rotary_low(u, i):
                a, c = i // 2, i % 2
                wait(pool, h_ready, 4 * u + i + 1)
                pool.tensor_tensor(out=rot[a][1][:, CH * c:CH * c + CH], in0=t1[:, i % 3, :],
                                   in1=rot[a][0][:, CH * c:CH * c + CH].bitcast(F32),
                                   op=ALU.subtract).then_inc(l_ready, 1)

            for i in range(4):
                rotary_sum(0, i)
                rotary_low(0, i)

            def unit(u, p, g, first, last):
                for s in range(8):
                    c, j = s // 4, s % 4
                    if s == 1:
                        if first:
                            pool.wait_ge(vsd, NT)
                        else:
                            wait(pool, pv_done, pv_before(u))
                        own(pool)
                        pool.tensor_copy(vals0[:, :, :, :], vals[:, T // P * p:T // P * p + KT,
                                                                 bass.ds(g * HG, HG), :]).then_inc(v0_ok, 1)
                    if s == 4:
                        if not first:
                            wait(pool, pv_done, pv_before(u) + 2 * KT)
                        own(pool)
                        pool.tensor_copy(vals1[:, :, :, :], vals[:, T // P * p:T // P * p + 2 * KT,
                                                                 bass.ds(g * HG, HG), :]).then_inc(v1_ok, 1)
                    for d in range(-1, KT):
                        if not last:
                            for what, i in {(1, -1): [(0, 0)], (1, 2): [(1, 0)], (2, -1): [(0, 1)], (2, 2): [(1, 1)],
                                            (3, -1): [(0, 2)], (3, 2): [(1, 2)], (4, -1): [(0, 3)],
                                            (4, 0): [(1, 3)]}.get((s, d), ()):
                                (rotary_sum, rotary_low)[what](u + 1, i)
                        if d < 0:
                            continue
                        kt = c * KT + d
                        wait(pool, exp_done, PER_UNIT * u + before(c, j) + kt + 1)
                        own(pool)
                        tri = probs[c][:, j, p_off(c, kt):p_off(c, kt) + P]
                        pool.affine_select(out=tri, in_=tri, compare_op=ALU.is_ge, fill=0.0, base=0,
                                           pattern=[[1, P]], channel_multiplier=-1).then_inc(masked, 1)

            unit_loop(pool, unit)

        @block.scalar
        def _(act):
            act.wait_ge(consts, 8)
            for i in range(4):
                act.wait_ge(mvd, 4 * i + 4)
                act.activation(rstd[:, 4 * i:4 * i + 4], mv[:, 4 * i:4 * i + 4, 1], ACT.Sqrt,
                               bias=eps[:, 0:1]).then_inc(rsd, 1)
            for i in range(4):
                act.wait_ge(tpd, i + 1)
                act.activation(xnT[:, CH * i:CH * i + CH], bank[i][:, :], ACT.Copy).then_inc(xnTd, 1)
            for i in range(4):
                act.wait_ge(qkvd, i + 1)
                act.activation(kvc[RQ:RQ + RKV, CH * i:CH * i + CH], bank[4 + i][RQ:RQ + RKV, :],
                               ACT.Copy).then_inc(kvcd, 1)
                act.activation(kvq[RQ:RQ + RKV, CH * i:CH * i + CH], bank[4 + i][RQ:RQ + RKV, :],
                               ACT.Square).then_inc(kvcd, 1)
                act.activation(qcT[:, CH * i:CH * i + CH], bank[4 + i][0:RQ, :], ACT.Copy).then_inc(qcd, 1)
            act.wait_ge(msd, 1)
            act.activation(krs[:, :], bank[0][:, 0:NT], ACT.Sqrt, bias=eps[:, 1:2]).then_inc(kr_in, 1)
            for i in range(4):
                for a in range(2):
                    act.wait_ge(cond, 2 * i + a + 1)
                    if i:
                        act.wait_ge(con_st[a], 48 * i)
                    act.activation(con_h[a].bitcast(F32R), bank[(4 * a + i)][:, :], ACT.Copy).then_inc(conh, 1)
            for i in range(4):
                act.wait_ge(vpd, i + 1)
                if i == 0:
                    act.wait_ge(consts, 8)
                act.activation(vals[:, KT * i:KT * i + KT, :, 0:DH],
                               bank[i][:, :].rearrange("p (t h d) -> p t h d", t=KT, h=H),
                               ACT.Copy).then_inc(vsd, 4)

            def high(u, p, i):
                a, c = i // 2, i % 2
                wait(act, s_ready, 4 * u + i + 1)
                if not isinstance(u, int) or u > 0:
                    for j in range(HG):
                        wait(act, ld_stk[1 - p][j], 48 * (u + p))
                act.activation(rot[a][0][:, CH * c:CH * c + CH], t1[:, i % 3, :], ACT.Copy).then_inc(h_ready, 1)

            for i in range(4):
                high(0, 0, i)

            def max_copy(u, c, j):
                n = HG * c + j
                wait(act, mt_done, 8 * u + n + 1)
                wait(act, ld_m[(j - 2) % HG], 32 * u + 16 * c + (16 if j >= 2 else 0))
                act.activation(mrow[:, j % 2, :], MT[0:KT, 0:P], ACT.Copy, scale=-1.0).then_inc(mrow_ok, 1)

            def max_row(u, p, c, j):
                wait(act, mrow_ok, 8 * u + HG * c + j + 1)
                act.dma_start(qs[p][QK:QK + 1, j, CH * c:CH * c + CH].bitcast(F32),
                              mrow[:, j % 2, :].bitcast(F32)).then_inc(ld_m[j], 16)

            def weigh(u, c, j, kt):
                k = PER_UNIT * u + before(c, j) + kt
                d = kt - c * KT
                width = CH if d < 0 else DIAG[d]
                at = P if d == KT - 1 else 0
                wait(act, st_done, k + 1)
                if not (isinstance(u, int) and u == 0):
                    wait(act, pv_done, (pv_before(u) - KT if c == 0 else pv_before(u)) + kt + 1)
                act.activation(probs[c][:, j, p_off(c, kt):p_off(c, kt) + width],
                               ST[(before(c, j) + kt) % 3][:, at:at + width], ACT.Exp,
                               scale=SCALE).then_inc(exp_done, 1)

            def pv_copy(n, k, turned):
                wait(act, pv_done, k)
                if turned is not None:
                    wait(act, wk_full, turned)
                act.activation(oT[:, n, :], PV[:, :], ACT.Copy).then_inc(pv_read, 1)

            for m in range(2):
                max_copy(0, 0, m)
                max_row(0, 0, 0, m)

            def unit(u, p, g, first, last):
                for s in range(ITEMS):
                    c, j = s // HG, s % HG
                    pending = None
                    if s == HG and not first:
                        pv_copy(1, pv_before(u) + 2 * KT, wk_before(u))
                    for k in range(SLOTS):
                        for kt in SCORES[c][k]:
                            weigh(u, c, j, kt)
                            if pending:
                                max_row(*pending)
                                pending = None
                        _, _, m, nxt = plan(s, k)
                        if m is not None and not (nxt and last):
                            v, pv = (u + 1, 1 - p) if nxt else (u, p)
                            max_copy(v, m // HG, m % HG)
                            if k == SLOTS - 1:
                                max_row(v, pv, m // HG, m % HG)
                            else:
                                pending = (v, pv, m // HG, m % HG)
                        i = {(1, 3): 0, (2, 3): 1, (3, 3): 2, (4, 2): 3}.get((s, k))
                        if i is not None and not last:
                            high(u + 1, 1 - p, i)
                    if pending:
                        max_row(*pending)
                    if s == ITEMS - 1:
                        pv_copy(0, pv_before(u) + (2 * KT if not first else 0) + KT,
                                None if first else wk_before(u) + (1 if last else 9))

            unit_loop(act, unit)
            pv_copy(1, pv_before(UNITS) + 2 * KT, wk_before(UNITS - 1) + 2)

        @block.vector
        def _(dve):
            dve.sem_inc(att_ok, 1)
            for p in range(2):
                dve.memset(ks[p][96:P, :, :].bitcast(F32), 1.0).then_inc(ks_ones, 1)
            for i in range(4):
                dve.wait_ge(ld_x[i], 16)
                for t in range(4 * i, 4 * i + 4):
                    dve.bn_stats(stats[:, t, :], xs[:, t, :]).then_inc(bnd, 1)
                for t in range(4 * i, 4 * i + 4):
                    dve.wait_ge(bnd, t + 1)
                    dve.bn_aggr(mv[:, t, :], stats[:, t, :]).then_inc(mvd, 1)
            for i in range(4):
                dve.wait_ge(rsd, i + 1)
                dve.reciprocal(rstd[:, 4 * i:4 * i + 4], rstd[:, 4 * i:4 * i + 4]).then_inc(rrd, 1)
                dve.wait_ge(rrd, i + 1)
                for t in range(4 * i, 4 * i + 4):
                    dve.tensor_scalar(xn[:, t, :], xs[:, t, :], mv[:, t, 0:1], rstd[:, t:t + 1],
                                      ALU.subtract, ALU.mult).then_inc(xnd, 1)
            dve.wait_ge(ld_w, 16 * 5)
            dve.tensor_scalar(wkd[RQ:RQ + RKV, :], wkd[RQ:RQ + RKV, :], gkv[RQ:RQ + RKV, 0:1], None,
                              ALU.mult).then_inc(gscaled, 1)
            dve.tensor_scalar(wvd[RQ:RQ + RKV, :], wvd[RQ:RQ + RKV, :], gkv[RQ:RQ + RKV, 0:1], None,
                              ALU.mult).then_inc(gscaled, 1)
            dve.wait_ge(kr_in, 1)
            dve.reciprocal(krs[:, :], krs[:, :]).then_inc(krd, 1)
            dve.wait_ge(krd, 1)
            dve.tensor_copy(krb.rearrange("p (t m) -> p t m", m=RKV),
                            krs[:, :].rearrange("p (t o) -> p t o", o=1).to_broadcast([P, NT, RKV]))\
               .then_inc(krd, 1)
            for i in range(4):
                c = slice(CH * i, CH * i + CH)
                dve.wait_ge(rbd, i + 1)
                dve.tensor_tensor(out=kvn[RQ:RQ + RKV, c], in0=bank[i][RQ:RQ + RKV, :],
                                  in1=kvc[RQ:RQ + RKV, c], op=ALU.mult).then_inc(kvnd, 1)
            for i in range(4):
                for a in range(2):
                    dve.wait_ge(conh, 2 * i + a + 1)
                    dve.tensor_tensor(out=con_l[a].bitcast(F32R), in0=bank[(4 * a + i)][:, :], in1=con_h[a],
                                      op=ALU.subtract).then_inc(conl, 1)
            dve.memset(PV[:, :], 0.0).then_inc(ks_ones, 1)
            dve.wait_ge(ld_tab, 32)

            def rotate(u, base, i, k):
                c = i % 2
                dst, tab = ((t1[:, i % 3, :], cos), (t2[:, i % 2, :], sin))[k]
                wait(dve, wk_full, base + 2 * i + k + 1)
                if k == 0:
                    wait(dve, l_ready, 4 * u + (0, -2, -1, 1)[i])
                else:
                    wait(dve, s_ready, 4 * u + i - 1)
                dve.tensor_tensor(out=dst, in0=WK[:, :], in1=tab[:, CH * c:CH * c + CH],
                                  op=ALU.mult).then_inc(wk_free, 1)

            for i in range(4):
                for k in range(2):
                    rotate(0, 0, i, k)

            def row_max(u, c, j, k):
                count = PER_UNIT * u + before(c, j) + k
                n = j
                t, whole = (k // 2, k % 2 == 0) if c else (k, False)
                width = P * (t + 1)
                wait(dve, mx_done, count + 1)
                if k == 0:
                    wait(dve, mt_done, 8 * u + HG * c + j - 3)
                if whole:
                    dve.tensor_reduce(m4[:, n, t:t + 1], MX[0][:, :], mybir.AxisListType.X, ALU.max)\
                       .then_inc(mx_read, 1)
                    return
                if c:
                    wait(dve, mx_read, count)
                own(dve)
                dve.tensor_tensor_reduce(MX[k % 2][:, 0:width], MX[k % 2][:, 0:width],
                                         mask[:, CH - width:CH], 1.0, m4[:, n, t:t + 1] if c else NEG,
                                         ALU.add, ALU.max, m4[:, n, t:t + 1]).then_inc(mx_read, 1)

            def normalise(u, c, w):
                o = WK[:, :].rearrange("p (t j v) -> p t j v", t=KT, j=HG)
                wait(dve, wk_full, w)
                wait(dve, att_ok, 1 + 2 * u + c)
                dve.reciprocal(rec[:, :, :], o[:, :, :, DH]).then_inc(rec_ok, 1)
                wait(dve, rec_ok, 2 * u + c + 1)
                wait(dve, att_st[c], 16 * (1 + u))
                dve.tensor_tensor(out=att[:, c, :, :].rearrange("p t (j v) -> p t j v", j=HG),
                                  in0=o[:, :, :, 0:DH],
                                  in1=rec[:, :, :].rearrange("p t (j o) -> p t j o", o=1)
                                  .to_broadcast([P, KT, HG, DH]), op=ALU.mult).then_inc(att_ok, 1)

            for n in range(LEAD):
                m, k = chunk_of(n)
                row_max(0, 0, m, k)

            def unit(u, p, g, first, last):
                for s in range(ITEMS):
                    for k in range(SLOTS):
                        nxt, n, _, _ = plan(s, k)
                        if not (nxt and last):
                            m, i = chunk_of(n)
                            row_max(u + 1 if nxt else u, m // HG, m % HG, i)
                        q = PRODUCTS.get((s, k - 1))
                        if q is not None and not last:
                            rotate(u + 1, wk_before(u), q // 2, q % 2)
                        if k == 3 and s in (4, 5) and not first:
                            normalise(u - 1, s - 4, wk_before(u) + (0 if last else 8) + s - 3)

            unit_loop(dve, unit)
            for c in range(NC):
                normalise(UNITS - 1, c, wk_before(UNITS - 1) + 2 + c + 1)

        @block.tensor
        def _(pe):
            pe.wait_ge(consts, 8)
            for i in range(4):
                for t in range(4):
                    pe.wait_ge(xnd, 4 * i + t + 1)
                    tr = pe.transpose(bank[i][:, P * t:P * t + P], xn[:, 4 * i + t, :], ident[:, :])
                tr.then_inc(tpd, 1)
            pe.wait_ge(ld_w, 16 * 5)
            for i in range(4):
                pe.wait_ge(xnTd, i + 1)
                pe.matmul(bank[4 + i][0:RQ + RKV, :], wqkv[:, :], xnT[:, CH * i:CH * i + CH],
                          start=True, stop=True).then_inc(qkvd, 1)
            kv = slice(RQ, RQ + RKV)
            for i in range(4):
                pe.wait_ge(kvcd, 2 * i + 2)
                for t in range(4 * i, 4 * i + 4):
                    mm = pe.matmul(bank[0][:, t:t + 1], kvq[kv, P * t:P * t + P], ones[kv, 0:1],
                                   start=True, stop=True)
            mm.then_inc(msd, 1)
            pe.wait_ge(krd, 2)
            for i in range(4):
                for t in range(4 * i, 4 * i + 4):
                    mm = pe.matmul(bank[i][kv, P * (t % 4):P * (t % 4) + P], krb[:, RKV * t:RKV * t + RKV],
                                   ident[:, :], start=True, stop=True)
                mm.then_inc(rbd, 1)
            pe.wait_ge(gscaled, 2)
            for i in range(4):
                c = slice(CH * i, CH * i + CH)
                pe.wait_ge(kvnd, i + 1)
                pe.matmul(bank[i][:, :], wkd[kv, :], kvn[kv, c], start=True, stop=True).then_inc(cond, 1)
                pe.wait_ge(qcd, i + 1)
                pe.matmul(bank[4 + i][:, :], wqd[:, :], qcT[:, c], start=True, stop=True).then_inc(cond, 1)
            for i in range(4):
                pe.wait_ge(conl, 2 * i + 1)
                for t in range(4):
                    mm = pe.matmul(bank[i][:, P * t:P * t + P], kvn[kv, CH * i + P * t:CH * i + P * t + P],
                                   wvd[kv, :], start=True, stop=True)
                mm.then_inc(vpd, 1)

            def project(u, p, g, i, k):
                a, c = i // 2, i % 2
                if i == 0 and k == 0:
                    wait(pe, ld_wr, 32 * (g + 1))
                    wait(pe, att_ok, 1 + 2 * (u - 2))
                wait(pe, wk_free, 8 * u + 2 * i + k)
                weights, latent = ((wkr, xnT), (wqr, qcT))[a]
                pe.matmul(WK[:, :], weights[:, k, :], latent[:, T * p + CH * c:T * p + CH * c + CH],
                          start=True, stop=True).then_inc(wk_full, 1)

            pe.wait_ge(conl, 8)
            for i in range(4):
                for k in range(2):
                    project(0, 0, 0, i, k)

            def max_chunk(u, p, c, j, k):
                n = PER_UNIT * u + before(c, j) + k
                t, half = (k, 0) if c == 0 else (k // 2, k % 2)
                width = CH if c and half == 0 else max(P * (t + 1), 2 * P)
                if k == 0 and c == 0:
                    if j == 0:
                        wait(pe, ld_con[p], 16 * (u - p) + 32)
                    wait(pe, ld_stk[p][j], 48 * (u - p) + 96)
                wait(pe, mx_read, n - 1)
                q0 = CH * c + P * t
                k0 = CH * half
                pe.matmul(MX[k % 2][:, 0:width], qs[p][0:QK, j, q0:q0 + P], ks[p][0:QK, j, k0:k0 + width],
                          start=True, stop=True).then_inc(mx_done, 1)

            def turn_max(u, c, j):
                n = HG * c + j
                wait(pe, mx_read, PER_UNIT * u + before(c, j) + WORK[c])
                wait(pe, mrow_ok, 8 * u + n)
                pe.transpose(MT[0:KT, 0:P], m4[:, j, :], ident[:, :]).then_inc(mt_done, 1)

            def score(u, p, c, j, kt):
                n = PER_UNIT * u + before(c, j) + kt
                d = kt - c * KT
                width = CH if d < 0 else max(DIAG[d], 2 * P)
                if kt == 0:
                    wait(pe, ld_m[j], 32 * u + 16 * (c + 1))
                wait(pe, exp_done, n - 2)
                q0 = CH * c + CH - width
                pe.matmul(ST[(before(c, j) + kt) % 3][:, 0:width], ks[p][0:QK + 1, j, P * kt:P * kt + P],
                          qs[p][0:QK + 1, j, q0:q0 + width], start=True, stop=True).then_inc(st_done, 1)

            def quad(u, c, kt, vals_c):
                d = kt - c * KT
                width = CH if d < 0 else DIAG[d]
                if kt == 0:
                    wait(pe, v1_ok if c else v0_ok, u + 1)
                    wait(pe, pv_read, 2 * u + c)
                wait(pe, exp_done, PER_UNIT * u + before(c, HG - 1) + kt + 1)
                if d >= 0:
                    wait(pe, masked, 2 * HG * KT * u + HG * KT * c + KT * (HG - 1) + d + 1)
                for j in range(HG):
                    mm = pe.matmul(PV[32 * j:32 * j + VW, CH - width:CH], vals_c[:, kt, j, :],
                                   probs[c][:, j, p_off(c, kt):p_off(c, kt) + width],
                                   start=(kt == 0), stop=(kt == WORK[c] - 1))
                mm.then_inc(pv_done, 1)

            def turn_sums(u, n):
                wait(pe, pv_read, 2 * u + n + 1)
                wait(pe, wk_free, 8 * (u + 3) if not isinstance(u, int) or u < UNITS - 2 else 8 * UNITS)
                wait(pe, att_ok, 1 + 2 * u + n)
                for t in range(KT):
                    tr = pe.transpose(WK[:, P * t:P * t + P], oT[:, n, P * t:P * t + P], ident[:, :])
                tr.then_inc(wk_full, 1)

            pe.wait_ge(vsd, NT)
            pe.wait_ge(ks_ones, 3)
            for n in range(LEAD):
                m, k = chunk_of(n)
                max_chunk(0, 0, 0, m, k)
                if n in (5, 9):
                    turn_max(0, 0, (n - 5) // 4)

            def unit(u, p, g, first, last):
                g1 = g if p == 0 else g + 1
                for s in range(ITEMS):
                    c, j = s // HG, s % HG
                    for k in range(SLOTS):
                        for kt in SCORES[c][k]:
                            score(u, p, c, j, kt)
                        nxt, n, m, turn_nxt = plan(s, k)
                        if not (nxt and last):
                            i, kk = chunk_of(n)
                            max_chunk(u + 1 if nxt else u, 1 - p if nxt else p, i // HG, i % HG, kk)
                        if m is not None and not (turn_nxt and last):
                            turn_max(u + 1 if turn_nxt else u, m // HG, m % HG)
                        q = PRODUCTS.get((s, k))
                        if q is not None and not last:
                            project(u + 1, 1 - p, g1, q // 2, q % 2)
                        if k == 2 and s in (4, 5) and not first:
                            turn_sums(u - 1, s - 4)
                        if k in (1, 4) and s < 4 and not first:
                            quad(u - 1, 1, 2 * s + k // 3, vals1)
                        if k == 3 and s >= 4:
                            quad(u, 0, s - 4, vals0)

            unit_loop(pe, unit)
            for kt in range(2 * KT):
                quad(UNITS - 1, 1, kt, vals1)
            for c in range(NC):
                turn_sums(UNITS - 1, c)


def mixture(nc, x, attn, w_o, router, gate_up, down, out):
    wte_d = nc.dram_tensor("wte", (P, P), F32, kind="Internal").ap()
    with ExitStack() as ctx:
        def sb(name, shape, dt=F32):
            return ctx.enter_context(nc.sbuf_tensor(name, shape, dt))

        def sem(name):
            return ctx.enter_context(nc.semaphore(name))

        y1 = sb("y1", [P, NT, D])
        at = sb("at_nat", [P, NT, D])
        attT = sb("attT", [P, B * T])
        xn2 = sb("xn2", [P, NT, D])
        x2T = sb("x2T", [P, B * T])
        xh = sb("xh", [P, B * T], F32R)
        xl = sb("xl", [P, B * T], F32R)
        wo = sb("wo", [P, D])
        rw = sb("rw", [P, E])
        ident2 = sb("ident2", [P, P])
        eps2 = sb("eps2", [P, 1])
        rev = sb("rev", [P, NT, E])
        stats2 = sb("stats2", [P, NT, 6])
        mv2 = sb("mv2", [P, NT, 2])
        rstd2 = sb("rstd2", [P, NT])
        lg, pr, eq, o1, p2, o2, wte = [sb(n, [P, NT, E]) for n in ("lg", "pr", "eq", "o1", "p2", "o2", "wte_s")]
        mx, sm, m1, f1, m2, f2 = [sb(n, [P, NT]) for n in ("mx", "sm", "m1", "f1", "m2", "f2")]
        wteT = sb("wteT", [P, P])
        raw = [sb(f"raw{p}", [P, WC]) for p in range(2)]
        wh = [sb(f"wh{p}", [P, WC], F32R) for p in range(2)]
        wl = [sb(f"wl{p}", [P, WC], F32R) for p in range(2)]
        wb = [sb(f"wb{p}", [P, B * T]) for p in range(2)]
        sg = sb("sg", [P, 2, CH])
        hf = sb("hf", [P, 2, CH])
        hh = sb("hh", [P, 2, len(IT), CH], F32R)
        hl = sb("hl", [P, 2, len(IT), CH], F32R)
        yw = sb("yw", [P, 2, CH])
        acc = sb("acc", [P, B * T])
        bank = [ctx.enter_context(nc.psum_tensor(f"mbank{i}", [P, CH], F32)) for i in range(8)]
        GB, UB, YB = bank[0:2], bank[2:4], bank[4:6]

        ld_at = [sem(f"ld_at{i}") for i in range(NB)]
        ld_y = sem("ld_y")
        ld_wo = sem("ld_wo")
        ld_raw = [sem(f"ld_raw{p}") for p in range(2)]
        ld_wb = [sem(f"ld_wb{p}") for p in range(2)]
        const2 = sem("const2")
        at_turned = sem("at_turned")
        attT_ok = sem("attT_ok")
        wo_done = sem("wo_done")
        y1_ok = sem("y1_ok")
        bn_ok = sem("bn_ok")
        mv_ok = sem("mv_ok")
        sq_ok = sem("sq_ok")
        rs_ok = sem("rs_ok")
        xn2_ok = sem("xn2_ok")
        x_turned = sem("x_turned")
        xh_ok = sem("xh_ok")
        x2T_ok = sem("x2T_ok")
        xl_ok = sem("xl_ok")
        logit_ok = sem("logit_ok")
        route = sem("route")
        exp_ok = sem("exp_ok")
        wte_turned = sem("wte_turned")
        wteT_ok = sem("wteT_ok")
        wte_st = sem("wte_st")
        pad_ok = sem("pad_ok")
        wh_ok = sem("wh_ok")
        wl_ok = sem("wl_ok")
        g_full = sem("g_full")
        u_full = sem("u_full")
        silu_ok = sem("silu_ok")
        hid_ok = sem("hid_ok")
        hh_ok = sem("hh_ok")
        hl_ok = sem("hl_ok")
        y_full = sem("y_full")
        y_read = sem("y_read")
        acc_ok = sem("acc_ok")
        acc_turned = sem("acc_turned")
        out_ok = sem("out_ok")
        out_done = sem("out_done")
        sp_passed = sem("sp_passed2")

        block = ctx.enter_context(nc.Block())

        def wait(eng, s, v):
            if not isinstance(v, int) or v > 0:
                eng.wait_ge(s, v)

        def pair_loop(eng, pair):
            pair(0)
            with eng.Fori(1, E // 2 - 1) as k:
                pair(k)
            pair(E // 2 - 1)

        def is_last(k, p):
            return isinstance(k, int) and k == E // 2 - 1 and p == 1

        @block.sync
        def _(sp):
            for i in range(NB):
                sp.dma_start(at[:, KT * i:KT * i + KT, :], attn[:, KT * i:KT * i + KT, :]).then_inc(ld_at[i], 16)
            sp.dma_start(wo[:, :], w_o).then_inc(ld_wo, 16)
            sp.dma_start(y1[:, :, :], x).then_inc(ld_y, 16)
            sp.dma_start(rw[:, :], router).then_inc(ld_wo, 16)

            def load_weights(k, p):
                wait(sp, wl_ok, 2 * k + p - 1)
                if isinstance(k, int) and k == 0:
                    sp.wait_ge(pad_ok, 2)
                sp.sem_inc(sp_passed, 1)
                e = bass.ds(2 * k + p, 1)
                sp.dma_start(raw[p][:, 0:GU], gate_up[e, :, :]).then_inc(ld_raw[p], 16)
                for r in range(len(IT)):
                    sp.dma_start(raw[p][0:IT[r], GU + D * r:GU + D * r + D],
                                 down[e, P * r:P * r + IT[r], :]).then_inc(ld_raw[p], 16)

            def load_tokens(k, p):
                wait(sp, y_read, 4 * (2 * k + p - 1))
                sp.sem_inc(sp_passed, 1)
                src = wte_d.rearrange("(t e) n -> e t n", e=E)[bass.ds(2 * k + p, 1), :, :]
                sp.dma_start(wb[p][:, :].rearrange("p (t n) -> p t n", n=P),
                             src.to_broadcast([P, NT, P])).then_inc(ld_wb[p], 16)

            for p in range(2):
                load_weights(0, p)
            sp.wait_ge(wteT_ok, 1)
            sp.dma_start(wte_d, wteT[:, :]).then_inc(wte_st, 16)
            sp.wait_ge(wte_st, 16)
            for p in range(2):
                load_tokens(0, p)
            with sp.Fori(1, E // 2) as k:
                for p in range(2):
                    load_weights(k, p)
                    load_tokens(k, p)
            for i in range(NB):
                sp.wait_ge(out_ok, i + 1)
                sp.dma_start(out[:, KT * i:KT * i + KT, :], y1[:, KT * i:KT * i + KT, :]).then_inc(out_done, 16)
            sp.wait_ge(out_done, 16 * NB)

        @block.gpsimd
        def _(pool):
            pool.memset(ident2[:, :], 0.0).then_inc(const2, 1)
            pool.wait_ge(const2, 1)
            pool.affine_select(out=ident2[:, :], in_=ident2[:, :], compare_op=ALU.not_equal, fill=1.0, base=0,
                               pattern=[[-1, P]], channel_multiplier=1).then_inc(const2, 1)
            pool.memset(eps2[:, :], 1e-5).then_inc(const2, 1)
            for e in range(E):
                pool.memset(rev[:, :, e], float(E - e)).then_inc(const2, 1)
            pool.memset(acc[:, :], 0.0).then_inc(const2, 1)

            def low(n):
                k, p = n
                wait(pool, wh_ok, 2 * k + p + 1)
                pool.tensor_tensor(out=wl[p][:, :], in0=raw[p][:, :], in1=wh[p][:, :].bitcast(F32),
                                   op=ALU.subtract).then_inc(wl_ok, 1)

            def add(n, c):
                wait(pool, y_read, n + 1)
                wait(pool, acc_ok, n - NB + 1)
                pool.tensor_tensor(out=acc[:, CH * c:CH * c + CH], in0=acc[:, CH * c:CH * c + CH],
                                   in1=yw[:, c % 2, :], op=ALU.add).then_inc(acc_ok, 1)

            low((0, 0))
            pool.wait_ge(const2, E + 4)

            def pair(k):
                for p in range(2):
                    for c in range(NB):
                        n = NB * (2 * k + p) + c
                        if not isinstance(n, int) or n >= 2:
                            add(n - 2, (c - 2) % NB)
                        if c == 1 and not is_last(k, p):
                            low((k, 1) if p == 0 else (k + 1, 0))

            pair_loop(pool, pair)
            for c in (2, 3):
                add(NB * (E - 1) + c, c)

        @block.scalar
        def _(act):
            for i in range(NB):
                act.wait_ge(at_turned, i + 1)
                act.activation(attT[:, CH * i:CH * i + CH], bank[i][:, :], ACT.Copy).then_inc(attT_ok, 1)
            act.wait_ge(const2, E + 4)
            for i in range(NB):
                act.wait_ge(mv_ok, KT * i + KT)
                act.activation(rstd2[:, KT * i:KT * i + KT], mv2[:, KT * i:KT * i + KT, 1], ACT.Sqrt,
                               bias=eps2[:, 0:1]).then_inc(sq_ok, 1)
            for i in range(NB):
                c = slice(CH * i, CH * i + CH)
                act.wait_ge(x_turned, i + 1)
                act.activation(x2T[:, c], bank[i][:, :], ACT.Copy).then_inc(x2T_ok, 1)
                act.activation(xh[:, c], bank[i][:, :], ACT.Copy).then_inc(xh_ok, 1)
            act.wait_ge(route, 2)
            act.activation(pr[:, :, :], lg[:, :, :], ACT.Exp).then_inc(exp_ok, 1)

            def high_weights(k, p):
                wait(act, ld_raw[p], 64 * (k + 1))
                wait(act, y_full, NB * (2 * k + p - 1))
                act.activation(wh[p][:, :], raw[p][:, :], ACT.Copy).then_inc(wh_ok, 1)

            high_weights(0, 0)
            act.wait_ge(wte_turned, 1)
            act.activation(wteT[:, :], bank[7][:, 0:P], ACT.Copy).then_inc(wteT_ok, 1)

            def silu(m, i, b):
                wait(act, g_full, m + 1)
                wait(act, hid_ok, m - 1)
                act.activation(sg[0:IT[i], b, :], GB[b][0:IT[i], :], ACT.Silu).then_inc(silu_ok, 1)

            def high(m, n, i, b, bn):
                wait(act, hid_ok, m + 1)
                wait(act, y_full, n - 1)
                act.activation(hh[0:IT[i], bn, i, :], hf[0:IT[i], b, :], ACT.Copy).then_inc(hh_ok, 1)

            def pair(k):
                for p in range(2):
                    for c in range(NB):
                        n = NB * (2 * k + p) + c
                        for i in range(3):
                            m = 3 * n + i
                            b = (c + i) % 2
                            silu(m, i, b)
                            if i:
                                high(m - 1, n, i - 1, 1 - b, c % 2)
                            elif not isinstance(n, int) or n > 0:
                                high(m - 1, n - 1, 2, 1 - b, (c - 1) % 2)
                        if c == 1 and not is_last(k, p):
                            high_weights(*((k, 1) if p == 0 else (k + 1, 0)))

            pair_loop(act, pair)
            high(3 * NB * E - 1, NB * E - 1, 2, 1, 1)

        @block.vector
        def _(dve):
            def bc(v):
                return v[:, :].rearrange("p (t o) -> p t o", o=1).to_broadcast([P, NT, E])

            for p in range(2):
                dve.memset(raw[p][IT[2]:P, GU + 2 * D:WC], 0.0).then_inc(pad_ok, 1)
            dve.wait_ge(ld_y, 16)
            for i in range(NB):
                dve.wait_ge(wo_done, i + 1)
                part = y1[:, KT * i:KT * i + KT, :]
                dve.tensor_tensor(out=part, in0=bank[4 + i][:, :].rearrange("p (t c) -> p t c", c=D), in1=part,
                                  op=ALU.add).then_inc(y1_ok, 1)
                dve.wait_ge(y1_ok, i + 1)
                for t in range(KT * i, KT * i + KT):
                    dve.bn_stats(stats2[:, t, :], y1[:, t, :]).then_inc(bn_ok, 1)
                for t in range(KT * i, KT * i + KT):
                    dve.wait_ge(bn_ok, t + 1)
                    dve.bn_aggr(mv2[:, t, :], stats2[:, t, :]).then_inc(mv_ok, 1)
            for i in range(NB):
                dve.wait_ge(sq_ok, i + 1)
                dve.reciprocal(rstd2[:, KT * i:KT * i + KT], rstd2[:, KT * i:KT * i + KT]).then_inc(rs_ok, 1)
                dve.wait_ge(rs_ok, i + 1)
                for t in range(KT * i, KT * i + KT):
                    dve.tensor_scalar(xn2[:, t, :], y1[:, t, :], mv2[:, t, 0:1], rstd2[:, t:t + 1],
                                      ALU.subtract, ALU.mult).then_inc(xn2_ok, 1)
            for i in range(NB):
                c = slice(CH * i, CH * i + CH)
                dve.wait_ge(xh_ok, i + 1)
                dve.tensor_tensor(out=xl[:, c], in0=x2T[:, c], in1=xh[:, c].bitcast(F32),
                                  op=ALU.subtract).then_inc(xl_ok, 1)
            dve.wait_ge(logit_ok, 1)
            logits = bank[6][:, 0:NT * E].rearrange("p (t e) -> p t e", e=E)
            X = mybir.AxisListType.X
            done = 0

            def step(ins):
                nonlocal done
                ins.then_inc(route, 1)
                done += 1
                dve.wait_ge(route, done)

            step(dve.tensor_reduce(mx[:, :], logits, X, ALU.max))
            step(dve.tensor_tensor(out=lg[:, :, :], in0=logits, in1=bc(mx), op=ALU.subtract))
            dve.wait_ge(exp_ok, 1)
            step(dve.tensor_reduce(sm[:, :], pr[:, :, :], X, ALU.add))
            step(dve.reciprocal(sm[:, :], sm[:, :]))
            step(dve.tensor_tensor(out=pr[:, :, :], in0=pr[:, :, :], in1=bc(sm), op=ALU.mult))
            for src, m, f, o in ((pr, m1, f1, o1), (p2, m2, f2, o2)):
                step(dve.tensor_reduce(m[:, :], src[:, :, :], X, ALU.max))
                step(dve.tensor_tensor(out=eq[:, :, :], in0=src[:, :, :], in1=bc(m), op=ALU.is_equal))
                step(dve.tensor_tensor(out=eq[:, :, :], in0=eq[:, :, :], in1=rev[:, :, :], op=ALU.mult))
                step(dve.tensor_reduce(f[:, :], eq[:, :, :], X, ALU.max))
                step(dve.tensor_tensor(out=o[:, :, :], in0=eq[:, :, :], in1=bc(f), op=ALU.is_equal))
                if o is o1:
                    step(dve.scalar_tensor_tensor(out=p2[:, :, :], in0=o1[:, :, :], scalar=-2.0, in1=pr[:, :, :],
                                                  op0=ALU.mult, op1=ALU.add))
            step(dve.tensor_tensor(out=o2[:, :, :], in0=o2[:, :, :], in1=o1[:, :, :], op=ALU.add))
            step(dve.tensor_tensor(out=wte[:, :, :], in0=pr[:, :, :], in1=o2[:, :, :], op=ALU.mult))

            def hidden(m, i, b):
                wait(dve, u_full, m + 1)
                wait(dve, silu_ok, m + 1)
                wait(dve, hl_ok, m - 1)
                dve.tensor_tensor(out=hf[0:IT[i], b, :], in0=UB[b][0:IT[i], :], in1=sg[0:IT[i], b, :],
                                  op=ALU.mult).then_inc(hid_ok, 1)

            def low(m, i, b, bn):
                wait(dve, hh_ok, m + 1)
                dve.tensor_tensor(out=hl[0:IT[i], bn, i, :], in0=hf[0:IT[i], b, :],
                                  in1=hh[0:IT[i], bn, i, :].bitcast(F32), op=ALU.subtract).then_inc(hl_ok, 1)

            def weigh(n, c, p, k):
                wait(dve, y_full, n + 1)
                wait(dve, ld_wb[p], 16 * (k + 1))
                wait(dve, acc_ok, n - 1)
                dve.tensor_tensor(out=yw[:, c % 2, :], in0=YB[c % 2][:, :], in1=wb[p][:, CH * c:CH * c + CH],
                                  op=ALU.mult).then_inc(y_read, 1)

            def pair(k):
                for p in range(2):
                    for c in range(NB):
                        n = NB * (2 * k + p) + c
                        for i in range(3):
                            m = 3 * n + i
                            b = (c + i) % 2
                            hidden(m, i, b)
                            if i:
                                low(m - 1, i - 1, 1 - b, c % 2)
                            elif not isinstance(n, int) or n > 0:
                                low(m - 1, 2, 1 - b, (c - 1) % 2)
                            if i == 0 and (not isinstance(n, int) or n > 1):
                                if c >= 2:
                                    weigh(n - 2, c - 2, p, k)
                                else:
                                    weigh(n - 2, c + 2, 1 - p, k if p else k - 1)

            pair_loop(dve, pair)
            low(3 * NB * E - 1, 2, 1, 1)
            for c in (2, 3):
                weigh(NB * (E - 1) + c, c, 1, E // 2 - 1)
            for i in range(NB):
                dve.wait_ge(acc_turned, i + 1)
                part = y1[:, KT * i:KT * i + KT, :]
                dve.tensor_tensor(out=part, in0=bank[i][:, :].rearrange("p (t c) -> p t c", c=D), in1=part,
                                  op=ALU.add).then_inc(out_ok, 1)

        @block.tensor
        def _(pe):
            pe.wait_ge(const2, 3)
            for i in range(NB):
                pe.wait_ge(ld_at[i], 16)
                for t in range(KT):
                    tr = pe.transpose(bank[i][:, P * t:P * t + P], at[:, KT * i + t, :], ident2[:, :])
                tr.then_inc(at_turned, 1)
            pe.wait_ge(ld_wo, 32)
            for i in range(NB):
                pe.wait_ge(attT_ok, i + 1)
                for t in range(KT):
                    q = CH * i + P * t
                    mm = pe.matmul(bank[4 + i][:, P * t:P * t + P], attT[:, q:q + P], wo[:, :], start=True, stop=True)
                mm.then_inc(wo_done, 1)
            for i in range(NB):
                for t in range(KT):
                    pe.wait_ge(xn2_ok, KT * i + t + 1)
                    tr = pe.transpose(bank[i][:, P * t:P * t + P], xn2[:, KT * i + t, :], ident2[:, :])
                tr.then_inc(x_turned, 1)
            for i in range(NB):
                pe.wait_ge(x2T_ok, i + 1)
                if i == 0:
                    pe.wait_ge(y1_ok, 3)
                for t in range(KT * i, KT * i + KT):
                    mm = pe.matmul(bank[6][:, E * t:E * t + E], x2T[:, P * t:P * t + P], rw[:, :],
                                   start=True, stop=True)
            mm.then_inc(logit_ok, 1)
            pe.wait_ge(y1_ok, NB)
            pe.wait_ge(xl_ok, NB)

            def split3(dst, w, v, k, start, stop):
                (w_h, w_l), (v_h, v_l) = w, v
                pe.matmul(dst, w_h, v_h, start=start, stop=False)
                pe.matmul(dst, w_h, v_l, start=False, stop=False)
                return pe.matmul(dst, w_l, v_h, start=False, stop=stop)

            def project(m, p, c, i, b):
                v = [s[:, CH * c:CH * c + CH] for s in (xh, xl)]
                wait(pe, silu_ok, m - 1)
                cols = slice(P * i, P * i + IT[i])
                split3(GB[b][0:IT[i], :], [w[p][:, cols] for w in (wh, wl)], v, P, True, True).then_inc(g_full, 1)
                wait(pe, hid_ok, m - 1)
                cols = slice(I + P * i, I + P * i + IT[i])
                split3(UB[b][0:IT[i], :], [w[p][:, cols] for w in (wh, wl)], v, P, True, True).then_inc(u_full, 1)

            def down_product(n, p, c, i):
                wait(pe, hl_ok, 3 * n + i + 1)
                if i == 0:
                    wait(pe, y_read, n - 1)
                r = slice(0, IT[i])
                cols = slice(GU + D * i, GU + D * i + D)
                mm = split3(YB[c % 2][:, :], [w[p][r, cols] for w in (wh, wl)],
                            [s[r, c % 2, i, :] for s in (hh, hl)], IT[i], i == 0, i == 2)
                if i == 2:
                    mm.then_inc(y_full, 1)

            def turn_wte():
                pe.wait_ge(route, 18)
                pe.transpose(bank[7][:, 0:P], wte[:, :, :].rearrange("p t e -> p (t e)"), ident2[:, :])\
                  .then_inc(wte_turned, 1)

            turn_wte()

            def pair(k):
                for p in range(2):
                    for c in range(NB):
                        n = NB * (2 * k + p) + c
                        if c == 0:
                            wait(pe, wl_ok, 2 * k + p + 1)
                        for i in range(3):
                            project(3 * n + i, p, c, i, (c + i) % 2)
                            if not isinstance(n, int) or n > 0:
                                down_product(n - 1, p if c else 1 - p, (c - 1) % NB, i)

            pair_loop(pe, pair)
            for i in range(3):
                down_product(NB * E - 1, 1, NB - 1, i)
            for i in range(NB):
                pe.wait_ge(acc_ok, NB * (E - 1) + i + 1)
                if i == 0:
                    pe.wait_ge(hid_ok, 3 * NB * E)
                for t in range(KT):
                    q = CH * i + P * t
                    tr = pe.transpose(bank[i][:, P * t:P * t + P], acc[:, q:q + P], ident2[:, :])
                tr.then_inc(acc_turned, 1)


def block_kernel(nc, x, w_qkv, w_kdec, w_vdec, w_qdec, g_kv, w_kr, w_qr, cosT, sinT, w_o, router, gate_up, down, out):
    attn = nc.dram_tensor("attn", (P, NT, H * DH), F32, kind="Internal").ap()
    attention(nc, x, w_qkv, w_kdec, w_vdec, w_qdec, g_kv, w_kr, w_qr, cosT, sinT, attn)
    mixture(nc, x, attn, w_o, router, gate_up, down, out)


def tables():
    inv_freq = 1.0 / 10000.0 ** (np.arange(0, R, 2, dtype=np.float32) / R)
    freqs = np.outer(np.arange(T, dtype=np.float32), inv_freq)
    emb = np.concatenate([freqs, freqs], -1).T
    sign = np.where(np.arange(R) < R // 2, -1.0, 1.0).astype(np.float32)[:, None]
    return np.tile(np.cos(emb), (HG, 1)), np.tile(np.sin(emb) * sign, (HG, 1))


def by_feature(w):
    return w.reshape(-1, H, DH).transpose(0, 2, 1).reshape(w.shape)


def partners(w):
    halves = w.reshape(w.shape[0], H, 2, R // 2)
    return np.stack([w, halves[:, :, ::-1].reshape(w.shape)], 1)


def kernel(**inputs):
    import concourse.bacc as bacc
    from concourse.bass_utils import run_bass_kernel_spmd

    a = {k: np.asarray(v) for k, v in inputs.items()}
    at, ff = "L0_attn_", "L0_ffn_"
    cos, sin = tables()
    ins = dict(
        x=a[at + "x"].reshape(NT, P, D).transpose(1, 0, 2),
        w_qkv=np.concatenate([a[at + "W_q"], a[at + "W_kv"]], 1),
        w_kdec=by_feature(a[at + "W_kdec"]), w_vdec=a[at + "W_vdec"], w_qdec=by_feature(a[at + "W_qdec"]),
        g_kv=a[at + "g_kv"][:, None],
        w_kr=partners(a[at + "W_krope"]), w_qr=partners(a[at + "W_qrope"]),
        cosT=cos, sinT=sin,
        w_o=a[at + "W_o"],
        router=a[ff + "router_w"].T,
        gate_up=np.concatenate([a[ff + "gate_w"].transpose(0, 2, 1), a[ff + "up_w"].transpose(0, 2, 1)], 2),
        down=a[ff + "down_w"].transpose(0, 2, 1),
    )
    ins = {k: np.ascontiguousarray(v) for k, v in ins.items()}
    nc = bacc.Bacc("TRN2", target_bir_lowering=False, num_devices=1)
    args = [nc.dram_tensor(k, v.shape, mybir.dt.from_np(v.dtype), kind="ExternalInput").ap() for k, v in ins.items()]
    out = nc.dram_tensor("out", (P, NT, D), F32, kind="ExternalOutput").ap()
    block_kernel(nc, *args, out)
    r = run_bass_kernel_spmd(nc, [ins], core_ids=[0])
    return np.asarray(r.results[0]["out"]).transpose(1, 0, 2).reshape(B, T, D)
```

```python
from contextlib import ExitStack

import numpy as np

import concourse.bass as bass
from concourse import mybir

F32 = mybir.dt.float32
F32R = mybir.dt.float32r
ALU = mybir.AluOpType
ACT = mybir.ActivationFunctionType

P = 128
B, T, D = 2, 1024, 128
NT = B * T // P
H, DH, R = 16, 8, 32
RKV, RQ = 32, 64
HG = 4
G = H // HG
UNITS = B * G
CH = 512
NC = T // CH
KT = CH // P
VW = DH + 1
QK = 3 * (R + DH)
SCALE = float(1.0 / np.sqrt(np.float32(DH + R)))
NEG = -3.0e38

DIAG = [CH - P * d for d in range(KT)]
PCOLS = [c * KT * CH + sum(DIAG) for c in range(NC)]


def p_off(c, kt):
    return kt * CH if kt < c * KT else c * KT * CH + sum(DIAG[:kt - c * KT])


WORK = [KT, 2 * KT]


def before(c, j):
    return c * HG * WORK[0] + j * WORK[c]


PER_UNIT = HG * sum(WORK)
ITEMS = NC * HG
SLOTS = PER_UNIT // ITEMS
LEAD = 2 * SLOTS + 1
SCORES = [[(0,), (1,), (), (2,), (3,), ()], [(0, 1), (2,), (3,), (4, 5), (6,), (7,)]]


def chunk_of(n):
    for m in range(ITEMS):
        c, j = m // HG, m % HG
        if n < before(c, j) + WORK[c]:
            return m, n - before(c, j)


def plan(s, k):
    n = LEAD + SLOTS * s + k
    nxt, n = n >= PER_UNIT, n % PER_UNIT
    last = n - 2 if n >= 2 else n - 2 + PER_UNIT
    m, i = chunk_of(last)
    turned = m if i == WORK[m // HG] - 1 else None
    return nxt, n, turned, nxt and n >= 2


PRODUCTS = {(q // 2, 3 * (q % 2)): q for q in range(8)}
QUADS = sum(WORK)

E, I = 8, 352
IT = [P, P, I - 2 * P]
GU = 2 * I
WC = GU + len(IT) * D
NB = B * T // CH


def attention(nc, x, w_qkv, w_kdec, w_vdec, w_qdec, g_kv, w_kr, w_qr, cosT, sinT, attn):
    con = nc.dram_tensor("content", (6, DH * H, B * T), F32, kind="Internal").ap()
    with ExitStack() as ctx:
        def sb(name, shape, dt=F32):
            return ctx.enter_context(nc.sbuf_tensor(name, shape, dt))

        def sem(name):
            return ctx.enter_context(nc.semaphore(name))

        xnT = sb("xnT", [P, B * T])
        qcT = sb("qcT", [2 * RQ, B * T], F32R)
        vals = sb("vals", [P, NT, H, VW])
        vals0 = sb("vals0", [P, KT, HG, VW])
        vals1 = sb("vals1", [P, 2 * KT, HG, VW])
        att = sb("att", [P, NC, KT, HG * DH])
        cos = sb("cos", [P, T])
        sin = sb("sin", [P, T])
        mask = sb("mask", [P, CH])
        ident = sb("ident", [P, P])
        gkv = sb("gkv", [P, 1])
        wkr = sb("wkr", [P, 2, P])
        wqr = sb("wqr", [2 * RQ, 2, P])
        wqh = sb("wqh", [2 * RQ, 2, P], F32R)
        wql = sb("wql", [RQ, 2, P], F32R)
        qs = [sb(f"qs{p}", [P, HG, T], F32R) for p in range(2)]
        ks = [sb(f"ks{p}", [P, HG, T], F32R) for p in range(2)]
        rot = [[sb(f"rot_{a}{p}", [P, T], F32R) for p in "hl"] for a in "kq"]
        t1 = sb("t1", [P, 3, CH])
        t2 = sb("t2", [P, CH])
        m4 = sb("m4", [P, HG, KT])
        mrow = sb("mrow", [KT, 2, P], F32R)
        oT = sb("oT", [P, 2, CH])
        rec = sb("rec", [P, KT, HG])
        probs = [sb(f"probs{c}", [P, HG, PCOLS[c]]) for c in range(NC)]
        rstd = sb("rstd", [P, NT])
        krs = sb("krs", [P, NT])
        eps = sb("eps", [P, 2])

        bank = [ctx.enter_context(nc.psum_tensor(f"bank{i}", [P, CH], F32)) for i in range(8)]
        MX, ST = bank[0:2], bank[2:5]
        PV, MT, WK = bank[5], bank[6], bank[7]

        ld_x = [sem(f"ld_x{i}") for i in range(4)]
        ld_w = sem("ld_w")
        ld_tab = sem("ld_tab")
        consts = sem("consts")
        gscaled = sem("gscaled")
        bnd = sem("bnd")
        mvd = sem("mvd")
        rsd = sem("rsd")
        rrd = sem("rrd")
        rbd = sem("rbd")
        xnd = sem("xnd")
        tpd = sem("tpd")
        xnTd = sem("xnTd")
        qkvd = sem("qkvd")
        kvcd = sem("kvcd")
        qcd = sem("qcd")
        msd = sem("msd")
        krd = sem("krd")
        kr_in = sem("kr_in")
        qch_ok = sem("qch_ok")
        qcl_ok = sem("qcl_ok")
        ld_qc = [sem(f"ld_qc{b}") for b in range(B)]
        wqh_ok = sem("wqh_ok")
        wql_ok = sem("wql_ok")
        kvnd = sem("kvnd")
        cond = sem("cond")
        conh = sem("conh")
        conl = sem("conl")
        vpd = sem("vpd")
        vsd = sem("vsd")
        con_st = [sem(f"con_st_{a}") for a in "kq"]
        ks_ones = sem("ks_ones")
        ld_wr = sem("ld_wr")
        wk_full = sem("wk_full")
        wk_free = sem("wk_free")
        s_ready = sem("s_ready")
        h_ready = sem("h_ready")
        l_ready = sem("l_ready")
        ld_con = [sem(f"ld_con{p}") for p in range(2)]
        ld_stk = [[sem(f"ld_stk{p}{j}") for j in range(HG)] for p in range(2)]
        att_st = [sem(f"att_st{c}") for c in range(NC)]
        att_ok = sem("att_ok")
        ld_m = [sem(f"ld_m{j}") for j in range(HG)]
        mx_done = sem("mx_done")
        mx_read = sem("mx_read")
        mt_done = sem("mt_done")
        mrow_ok = sem("mrow_ok")
        st_done = sem("st_done")
        exp_done = sem("exp_done")
        masked = sem("masked")
        pv_done = sem("pv_done")
        pv_read = sem("pv_read")
        v0_ok = sem("v0_ok")
        v1_ok = sem("v1_ok")
        rec_ok = sem("rec_ok")
        passed = {e.engine: sem(f"passed_{n}") for n, e in (("sp", nc.sync), ("pool", nc.gpsimd), ("dve", nc.vector))}

        block = ctx.enter_context(nc.Block())

        flat = probs[0][:, :, :].rearrange("p j c -> p (j c)")
        xs = flat[:, 0:NT * D].rearrange("p (t c) -> p t c", c=D)
        at = NT * D
        wqkv, wkd, wvd, wqd, ones = [flat[:, at + P * i:at + P * i + n]
                                     for i, n in enumerate((RQ + RKV, H * DH, H * DH, H * DH, RKV))]
        wqd = wqd[0:RQ, :]
        at += 5 * P
        qcf = flat[0:RQ, 0:B * T]
        qcl = flat[0:RQ, HG * PCOLS[0] - B * T:HG * PCOLS[0]]
        stats = flat[:, at:at + 6 * NT].rearrange("p (t c) -> p t c", c=6)
        mv = flat[:, at + 6 * NT:at + 8 * NT].rearrange("p (t c) -> p t c", c=2)
        flat = probs[1][:, :, :].rearrange("p j c -> p (j c)")
        xn = flat[:, 0:4 * CH].rearrange("p (t c) -> p t c", c=D)
        kvc = flat[:, 4 * CH:8 * CH]
        kvq = flat[:, 8 * CH:12 * CH]
        krb = flat[:, 12 * CH:13 * CH]
        kvn = flat[:, 16 * CH:20 * CH]
        con_h = [[flat[:, (20 + 2 * a + i) * CH:(21 + 2 * a + i) * CH] for i in range(2)] for a in range(2)]
        con_l = [[flat[:, (2 * a + i) * CH:(2 * a + i + 1) * CH] for i in range(2)] for a in range(2)]

        con_bank = [[bank[4 + i] for i in range(4)], [bank[i] for i in range(4)]]
        val_bank = [bank[4], bank[5], bank[0], bank[1]]

        def wait(eng, s, v):
            if not isinstance(v, int) or v > 0:
                eng.wait_ge(s, v)

        def own(eng):
            eng.sem_inc(passed[eng.engine], 1)

        def unit_loop(eng, unit):
            unit(0, 0, 0, True, False)
            with eng.Fori(0, G - 1) as i:
                u = eng.snap(2 * i + 1)
                unit(u, 1, i, False, False)
                unit(u + 1, 0, i + 1, False, False)
            unit(UNITS - 1, 1, G - 1, False, True)

        def wk_before(u):
            return 10 * u + 6 if not isinstance(u, int) or u > 0 else 8

        def pv_before(u):
            return QUADS * u - 2 * KT if not isinstance(u, int) or u > 0 else 0

        @block.sync
        def _(sp):
            for c in range(NC):
                sp.sem_inc(att_st[c], 16)
            for i in range(4):
                sp.dma_start(xs[:, 4 * i:4 * i + 4, :], x[:, 4 * i:4 * i + 4, :]).then_inc(ld_x[i], 16)
            sp.dma_start(wqkv[:, :], w_qkv).then_inc(ld_w, 16)
            sp.dma_start(wkd[RQ:RQ + RKV, :], w_kdec).then_inc(ld_w, 16)
            sp.dma_start(wvd[RQ:RQ + RKV, :], w_vdec).then_inc(ld_w, 16)
            sp.dma_start(wqd[:, :], w_qdec).then_inc(ld_w, 16)
            sp.dma_start(gkv[RQ:RQ + RKV, :], g_kv).then_inc(ld_w, 16)
            sp.dma_start(cos[:, :], cosT).then_inc(ld_tab, 16)
            sp.dma_start(sin[:, :], sinT).then_inc(ld_tab, 16)

            def load_rot(g):
                sp.dma_start(wkr[:, :, :], w_kr[:, :, bass.ds(g * P, P)]).then_inc(ld_wr, 16)
                sp.dma_start(wqr[:, :, :], w_qr[:, :, bass.ds(g * P, P)]).then_inc(ld_wr, 16)

            load_rot(0)

            def load_latents(i):
                sp.wait_ge(qcl_ok, i + 1)
                c = slice(CH * i, CH * i + CH)
                sp.dma_start(qcT[RQ:2 * RQ, c].bitcast(F32), qcl[:, c]).then_inc(ld_qc[i // NC], 16)

            load_latents(0)
            load_latents(1)

            def store_content(i):
                for a in range(2):
                    sp.wait_ge(conl, 2 * i + a + 1)
                    high_rows = (con[0:3:2], con[3:5])[a][:, :, CH * i:CH * i + CH].rearrange("k p t -> p k t")
                    sp.dma_start(high_rows, con_h[a][i % 2].rearrange("p (o t) -> p o t", o=1)
                                 .to_broadcast([P, 2, CH])).then_inc(con_st[a], 16)
                    sp.dma_start(con[(1, 5)[a], :, CH * i:CH * i + CH], con_l[a][i % 2]).then_inc(con_st[a], 16)

            def load_content(u, p, g):
                if not isinstance(u, int) or u > 1:
                    wait(sp, st_done, PER_UNIT * (u - 1))
                    own(sp)
                for a in range(2):
                    if isinstance(u, int) and u < 2:
                        sp.wait_ge(ks_ones, u + 1)
                        sp.wait_ge(con_st[a], 32 * 2 * (u + 1))
                    src = con[3 * a:3 * a + 3, :, T * p:T * p + T].rearrange("k (d h) t -> (k d) h t", h=H)
                    sp.dma_start((ks, qs)[a][p][3 * R:QK, :, :].bitcast(F32),
                                 src[:, bass.ds(g * HG, HG), :]).then_inc(ld_con[p], 16)

            def load_rotary(u, p, j, a):
                if j == 0:
                    own(sp)
                    wait(sp, l_ready, 4 * u + 2 * a + 2)
                for k, lo in enumerate(([0, 1, 0], [0, 0, 1])[a]):
                    sp.dma_start((ks, qs)[a][p][R * k:R * k + R, j, :].bitcast(F32),
                                 rot[a][lo][R * j:R * j + R, :].bitcast(F32)).then_inc(ld_stk[p][j], 16)

            def store_att(u, p, g, c):
                wait(sp, att_ok, 1 + 2 * u + c + 1)
                own(sp)
                sp.dma_start(attn[:, T // P * p + KT * c:T // P * p + KT * c + KT, bass.ds(g * (HG * DH), HG * DH)],
                             att[:, c, :, :]).then_inc(att_st[c], 16)

            for j in range(HG):
                load_rotary(0, 0, j, 0)
            store_content(0)
            store_content(1)
            load_rotary(0, 0, 0, 1)
            load_latents(2)
            load_latents(3)
            load_content(0, 0, 0)
            for j in range(1, HG):
                load_rotary(0, 0, j, 1)
            for i in (2, 3):
                store_content(i)

            def unit(u, p, g, first, last):
                g1, gb = (g, g - 1) if p == 0 else (g + 1, g)
                for s in range(ITEMS):
                    if s == 2 and not last:
                        load_content(u + 1, 1 - p, g1)
                    if s == 4 and p == 0:
                        wait(sp, wk_full, wk_before(u) + 8)
                        own(sp)
                        load_rot((g + 1) % G)
                    for h in range(2):
                        n = 2 * s + h - 5
                        if 0 <= n < 2 * HG and not last:
                            wait(sp, st_done, PER_UNIT * u + before(s // HG, s % HG) + h * WORK[s // HG] // 2)
                            load_rotary(u + 1, 1 - p, n % HG, n // HG)
                    if s in (5, 7) and not first:
                        store_att(u - 1, 1 - p, gb, (s - 5) // 2)

            unit_loop(sp, unit)
            for c in range(NC):
                store_att(UNITS - 1, 1, G - 1, c)
                sp.wait_ge(att_st[c], 16 * (1 + UNITS))

        @block.gpsimd
        def _(pool):
            pool.memset(ident[:, :], 0.0).then_inc(consts, 1)
            pool.memset(mask[:, :], 0.0).then_inc(consts, 1)
            pool.wait_ge(consts, 2)
            pool.affine_select(out=ident[:, :], in_=ident[:, :], compare_op=ALU.not_equal, fill=1.0, base=0,
                               pattern=[[-1, P]], channel_multiplier=1).then_inc(consts, 1)
            pool.affine_select(out=mask[:, CH - P:CH], in_=mask[:, CH - P:CH], compare_op=ALU.is_ge, fill=NEG,
                               base=0, pattern=[[-1, P]], channel_multiplier=1).then_inc(consts, 1)
            pool.memset(ones[:, :], 1.0 / RKV).then_inc(consts, 1)
            pool.memset(eps[:, 0:1], 1e-5).then_inc(consts, 1)
            pool.memset(eps[:, 1:2], 1e-6).then_inc(consts, 1)
            pool.memset(vals[:, :, :, :], 1.0).then_inc(consts, 1)
            pool.wait_ge(consts, 8)
            for p in range(2):
                if p:
                    pool.wait_ge(ks_ones, p)
                pool.memset(ks[p][96:P, :, :].bitcast(F32), 1.0).then_inc(ks_ones, 1)
            pool.wait_ge(ks_ones, 2)

            def rotary_sum(u, i):
                wait(pool, wk_free, 8 * u + 2 * i + 2)
                pool.tensor_tensor(out=t1[:, i % 3, :], in0=t1[:, i % 3, :], in1=t2[:, :],
                                   op=ALU.add).then_inc(s_ready, 1)

            def rotary_low(u, i):
                a, c = i // 2, i % 2
                wait(pool, h_ready, 4 * u + i + 1)
                pool.tensor_tensor(out=rot[a][1][:, CH * c:CH * c + CH], in0=t1[:, i % 3, :],
                                   in1=rot[a][0][:, CH * c:CH * c + CH].bitcast(F32),
                                   op=ALU.subtract).then_inc(l_ready, 1)

            def low_weights(n):
                wait(pool, wqh_ok, n)
                own(pool)
                pool.tensor_tensor(out=wql[:, :, :], in0=wqr[0:RQ, :, :], in1=wqh[0:RQ, :, :].bitcast(F32),
                                   op=ALU.subtract).then_inc(wql_ok, 1)

            def low_latents(i):
                c = slice(CH * i, CH * i + CH)
                pool.wait_ge(qch_ok, i + 1)
                pool.wait_ge(qcd, i + 1)
                pool.tensor_tensor(out=qcl[:, c].bitcast(F32R), in0=qcf[:, c], in1=qcT[0:RQ, c].bitcast(F32),
                                   op=ALU.subtract).then_inc(qcl_ok, 1)

            low_weights(1)
            for i in range(2):
                low_latents(i)
            for i in range(4):
                rotary_sum(0, i)
                rotary_low(0, i)
            for i in (2, 3):
                low_latents(i)

            def unit(u, p, g, first, last):
                for s in range(8):
                    c, j = s // 4, s % 4
                    if s == 1:
                        if first:
                            pool.wait_ge(vsd, NT)
                        else:
                            wait(pool, pv_done, pv_before(u))
                        own(pool)
                        pool.tensor_copy(vals0[:, :, :, :], vals[:, T // P * p:T // P * p + KT,
                                                                 bass.ds(g * HG, HG), :]).then_inc(v0_ok, 1)
                    if s == 6 and p == 0:
                        low_weights(g + 2)
                    if s == 4:
                        if not first:
                            wait(pool, pv_done, pv_before(u) + 2 * KT)
                        own(pool)
                        pool.tensor_copy(vals1[:, :, :, :], vals[:, T // P * p:T // P * p + 2 * KT,
                                                                 bass.ds(g * HG, HG), :]).then_inc(v1_ok, 1)
                    for d in range(-1, KT):
                        if not last:
                            for what, i in {(1, -1): [(0, 0)], (1, 2): [(1, 0)], (2, -1): [(0, 1)], (2, 2): [(1, 1)],
                                            (3, -1): [(0, 2)], (3, 2): [(1, 2)], (4, -1): [(0, 3)],
                                            (4, 0): [(1, 3)]}.get((s, d), ()):
                                (rotary_sum, rotary_low)[what](u + 1, i)
                        if d < 0:
                            continue
                        kt = c * KT + d
                        wait(pool, exp_done, PER_UNIT * u + before(c, j) + kt + 1)
                        own(pool)
                        tri = probs[c][:, j, p_off(c, kt):p_off(c, kt) + P]
                        pool.affine_select(out=tri, in_=tri, compare_op=ALU.is_ge, fill=0.0, base=0,
                                           pattern=[[1, P]], channel_multiplier=-1).then_inc(masked, 1)

            unit_loop(pool, unit)

        @block.scalar
        def _(act):
            act.wait_ge(consts, 8)
            for i in range(4):
                act.wait_ge(mvd, 4 * i + 4)
                act.activation(rstd[:, 4 * i:4 * i + 4], mv[:, 4 * i:4 * i + 4, 1], ACT.Sqrt,
                               bias=eps[:, 0:1]).then_inc(rsd, 1)
            for i in range(4):
                act.wait_ge(tpd, i + 1)
                act.activation(xnT[:, CH * i:CH * i + CH], bank[i][:, :], ACT.Copy).then_inc(xnTd, 1)

            def high_weights(n):
                wait(act, ld_wr, 32 * n)
                act.activation(wqh[:, :, :], wqr[:, :, :], ACT.Copy).then_inc(wqh_ok, 1)

            high_weights(1)
            for i in range(4):
                act.wait_ge(qkvd, i + 1)
                act.activation(kvc[RQ:RQ + RKV, CH * i:CH * i + CH], bank[4 + i][RQ:RQ + RKV, :],
                               ACT.Copy).then_inc(kvcd, 1)
                act.activation(kvq[RQ:RQ + RKV, CH * i:CH * i + CH], bank[4 + i][RQ:RQ + RKV, :],
                               ACT.Square).then_inc(kvcd, 1)
                act.activation(qcT[0:RQ, CH * i:CH * i + CH], bank[4 + i][0:RQ, :], ACT.Copy).then_inc(qch_ok, 1)
                act.activation(qcf[:, CH * i:CH * i + CH], bank[4 + i][0:RQ, :], ACT.Copy).then_inc(qcd, 1)
            act.wait_ge(msd, 1)
            act.activation(krs[:, :], bank[4][:, 0:NT], ACT.Sqrt, bias=eps[:, 1:2]).then_inc(kr_in, 1)
            def high(u, p, i):
                a, c = i // 2, i % 2
                wait(act, s_ready, 4 * u + i + 1)
                if not isinstance(u, int) or u > 0:
                    for j in range(HG):
                        wait(act, ld_stk[1 - p][j], 48 * (u + p))
                act.activation(rot[a][0][:, CH * c:CH * c + CH], t1[:, i % 3, :], ACT.Copy).then_inc(h_ready, 1)

            def content_high(i):
                for a in range(2):
                    act.wait_ge(cond, 2 * i + a + 1)
                    if i == 2:
                        act.wait_ge(con_st[a], 64)
                    act.activation(con_h[a][i % 2].bitcast(F32R), con_bank[a][i][:, :], ACT.Copy).then_inc(conh, 1)

            high(0, 0, 0)
            high(0, 0, 1)
            content_high(0)
            high(0, 0, 2)
            content_high(1)
            high(0, 0, 3)
            for i in range(4):
                act.wait_ge(vpd, i + 1)
                act.activation(vals[:, KT * i:KT * i + KT, :, 0:DH],
                               val_bank[i][:, :].rearrange("p (t h d) -> p t h d", t=KT, h=H),
                               ACT.Copy).then_inc(vsd, 4)
            content_high(2)
            content_high(3)

            def max_copy(u, p, c, j):
                n = HG * c + j
                wait(act, mt_done, 8 * u + n + 1)
                wait(act, ld_m[(j - 2) % HG], 32 * u + 16 * c + (16 if j >= 2 else 0))
                act.activation(mrow[:, j % 2, :], MT[0:KT, 0:P], ACT.Copy, scale=-1.0).then_inc(mrow_ok, 1)

            def max_row(u, p, c, j):
                wait(act, mrow_ok, 8 * u + HG * c + j + 1)
                act.dma_start(qs[p][QK:QK + 1, j, CH * c:CH * c + CH].bitcast(F32),
                              mrow[:, j % 2, :].bitcast(F32)).then_inc(ld_m[j], 16)

            def weigh(u, c, j, kt):
                k = PER_UNIT * u + before(c, j) + kt
                d = kt - c * KT
                width = CH if d < 0 else DIAG[d]
                at = P if d == KT - 1 else 0
                wait(act, st_done, k + 1)
                if not (isinstance(u, int) and u == 0):
                    wait(act, pv_done, (pv_before(u) - KT if c == 0 else pv_before(u)) + kt + 1)
                act.activation(probs[c][:, j, p_off(c, kt):p_off(c, kt) + width],
                               ST[(before(c, j) + kt) % len(ST)][:, at:at + width], ACT.Exp,
                               scale=SCALE).then_inc(exp_done, 1)

            def pv_copy(n, k, turned):
                wait(act, pv_done, k)
                if turned is not None:
                    wait(act, wk_full, turned)
                act.activation(oT[:, n, :], PV[:, :], ACT.Copy).then_inc(pv_read, 1)

            for m in range((LEAD - 2) // KT):
                max_copy(0, 0, 0, m)
                max_row(0, 0, 0, m)

            for b in range(B):
                act.wait_ge(ld_qc[b], 16 * NC)

            def unit(u, p, g, first, last):
                for s in range(ITEMS):
                    c, j = s // HG, s % HG
                    if s == HG and first:
                        for a in range(2):
                            act.wait_ge(con_st[a], 128)
                    if s == HG and not first:
                        pv_copy(1, pv_before(u) + 2 * KT, wk_before(u))
                    for k in range(SLOTS):
                        for kt in SCORES[c][k]:
                            weigh(u, c, j, kt)
                        for ago, what in ((2, max_row), (1, max_copy)):
                            at, slot = divmod(SLOTS * s + k - ago, SLOTS)
                            if at < 0 and first:
                                continue
                            _, _, m, nxt = plan(at, slot)
                            if m is not None and not (nxt and last):
                                v, pv = (u + 1, 1 - p) if nxt else (u, p)
                                what(v, pv, m // HG, m % HG)
                        if (s, k) == (6, 2) and p == 0:
                            high_weights(g + 2)
                        i = {(1, 3): 0, (2, 3): 1, (3, 3): 2, (4, 2): 3}.get((s, k))
                        if i is not None and not last:
                            high(u + 1, 1 - p, i)
                    if s == ITEMS - 1:
                        pv_copy(0, pv_before(u) + (2 * KT if not first else 0) + KT,
                                None if first else wk_before(u) + (1 if last else 9))

            unit_loop(act, unit)
            pv_copy(1, pv_before(UNITS) + 2 * KT, wk_before(UNITS - 1) + 2)

        @block.vector
        def _(dve):
            dve.sem_inc(att_ok, 1)
            for i in range(4):
                dve.wait_ge(ld_x[i], 16)
                for t in range(4 * i, 4 * i + 4):
                    dve.bn_stats(stats[:, t, :], xs[:, t, :]).then_inc(bnd, 1)
                for t in range(4 * i, 4 * i + 4):
                    dve.wait_ge(bnd, t + 1)
                    dve.bn_aggr(mv[:, t, :], stats[:, t, :]).then_inc(mvd, 1)
            for i in range(4):
                dve.wait_ge(rsd, i + 1)
                dve.reciprocal(rstd[:, 4 * i:4 * i + 4], rstd[:, 4 * i:4 * i + 4]).then_inc(rrd, 1)
                dve.wait_ge(rrd, i + 1)
                for t in range(4 * i, 4 * i + 4):
                    dve.tensor_scalar(xn[:, t, :], xs[:, t, :], mv[:, t, 0:1], rstd[:, t:t + 1],
                                      ALU.subtract, ALU.mult).then_inc(xnd, 1)
            dve.wait_ge(ld_w, 16 * 5)
            dve.tensor_scalar(wkd[RQ:RQ + RKV, :], wkd[RQ:RQ + RKV, :], gkv[RQ:RQ + RKV, 0:1], None,
                              ALU.mult).then_inc(gscaled, 1)
            dve.tensor_scalar(wvd[RQ:RQ + RKV, :], wvd[RQ:RQ + RKV, :], gkv[RQ:RQ + RKV, 0:1], None,
                              ALU.mult).then_inc(gscaled, 1)

            def rotate(u, base, i, k, src):
                c = i % 2
                dst, tab = ((t1[:, i % 3, :], cos), (t2[:, :], sin))[k]
                wait(dve, wk_full, base + 2 * i + k + 1)
                if k == 0:
                    wait(dve, l_ready, 4 * u + (0, -2, -1, 1)[i])
                else:
                    wait(dve, s_ready, 4 * u + i)
                dve.tensor_tensor(out=dst, in0=src[:, :], in1=tab[:, CH * c:CH * c + CH],
                                  op=ALU.mult).then_inc(wk_free, 1)

            dve.wait_ge(ld_tab, 32)
            for q in range(4):
                rotate(0, 0, q // 2, q % 2, bank[q % 4])
            dve.wait_ge(kr_in, 1)
            dve.reciprocal(krs[:, :], krs[:, :]).then_inc(krd, 1)
            dve.wait_ge(krd, 1)
            dve.tensor_copy(krb.rearrange("p (t m) -> p t m", m=RKV),
                            krs[:, :].rearrange("p (t o) -> p t o", o=1).to_broadcast([P, NT, RKV]))\
               .then_inc(krd, 1)
            for i in range(4):
                c = slice(CH * i, CH * i + CH)
                dve.wait_ge(rbd, i + 1)
                dve.tensor_tensor(out=kvn[RQ:RQ + RKV, c], in0=bank[4 + i][RQ:RQ + RKV, :],
                                  in1=kvc[RQ:RQ + RKV, c], op=ALU.mult).then_inc(kvnd, 1)

            def content_low(i):
                for a in range(2):
                    dve.wait_ge(conh, 2 * i + a + 1)
                    dve.tensor_tensor(out=con_l[a][i % 2].bitcast(F32R), in0=con_bank[a][i][:, :],
                                      in1=con_h[a][i % 2], op=ALU.subtract).then_inc(conl, 1)

            for q in range(4, 8):
                rotate(0, 0, q // 2, q % 2, bank[q % 4])
            for i in range(4):
                content_low(i)
            dve.wait_ge(vsd, NT)
            dve.memset(PV[:, :], 0.0).then_inc(ks_ones, 1)

            def row_max(u, c, j, k):
                count = PER_UNIT * u + before(c, j) + k
                n = j
                t, whole = (k // 2, k % 2 == 0) if c else (k, False)
                width = P * (t + 1)
                wait(dve, mx_done, count + 1)
                if k == 0:
                    wait(dve, mt_done, 8 * u + HG * c + j - 3)
                if whole:
                    dve.tensor_reduce(m4[:, n, t:t + 1], MX[(before(c, j) + k) % len(MX)][:, :],
                                      mybir.AxisListType.X, ALU.max)\
                       .then_inc(mx_read, 1)
                    return
                if c:
                    wait(dve, mx_read, count)
                own(dve)
                at = MX[(before(c, j) + k) % len(MX)][:, 0:width]
                dve.tensor_tensor_reduce(at, at,
                                         mask[:, CH - width:CH], 1.0, m4[:, n, t:t + 1] if c else NEG,
                                         ALU.add, ALU.max, m4[:, n, t:t + 1]).then_inc(mx_read, 1)

            def normalise(u, c, w):
                o = WK[:, :].rearrange("p (t j v) -> p t j v", t=KT, j=HG)
                wait(dve, wk_full, w)
                wait(dve, att_ok, 1 + 2 * u + c)
                dve.reciprocal(rec[:, :, :], o[:, :, :, DH]).then_inc(rec_ok, 1)
                wait(dve, rec_ok, 2 * u + c + 1)
                wait(dve, att_st[c], 16 * (1 + u))
                dve.tensor_tensor(out=att[:, c, :, :].rearrange("p t (j v) -> p t j v", j=HG),
                                  in0=o[:, :, :, 0:DH],
                                  in1=rec[:, :, :].rearrange("p t (j o) -> p t j o", o=1)
                                  .to_broadcast([P, KT, HG, DH]), op=ALU.mult).then_inc(att_ok, 1)

            for n in range(LEAD):
                m, k = chunk_of(n)
                row_max(0, 0, m, k)

            def unit(u, p, g, first, last):
                for s in range(ITEMS):
                    for k in range(SLOTS):
                        nxt, n, _, _ = plan(s, k)
                        if not (nxt and last):
                            m, i = chunk_of(n)
                            row_max(u + 1 if nxt else u, m // HG, m % HG, i)
                        q = PRODUCTS.get((s, k))
                        if q is not None and not last:
                            rotate(u + 1, wk_before(u), q // 2, q % 2, WK)
                        if k == 3 and s in (4, 5) and not first:
                            normalise(u - 1, s - 4, wk_before(u) + (0 if last else 8) + s - 3)

            unit_loop(dve, unit)
            for c in range(NC):
                normalise(UNITS - 1, c, wk_before(UNITS - 1) + 2 + c + 1)

        @block.tensor
        def _(pe):
            pe.wait_ge(consts, 8)
            for i in range(4):
                for t in range(4):
                    pe.wait_ge(xnd, 4 * i + t + 1)
                    tr = pe.transpose(bank[i][:, P * t:P * t + P], xn[:, 4 * i + t, :], ident[:, :])
                tr.then_inc(tpd, 1)
            pe.wait_ge(ld_w, 16 * 5)
            for i in range(4):
                pe.wait_ge(xnTd, i + 1)
                pe.matmul(bank[4 + i][0:RQ + RKV, :], wqkv[:, :], xnT[:, CH * i:CH * i + CH],
                          start=True, stop=True).then_inc(qkvd, 1)

            def project(p, i, k, dst):
                a, c = i // 2, i % 2
                t = slice(T * p + CH * c, T * p + CH * c + CH)
                if a == 0:
                    mm = pe.matmul(dst[:, :], wkr[:, k, :], xnT[:, t], start=True, stop=True)
                else:
                    pe.matmul(dst[:, :], wqh[:, k, :], qcT[:, t], start=True, stop=False)
                    mm = pe.matmul(dst[:, :], wql[:, k, :], qcT[0:RQ, t], start=False, stop=True)
                mm.then_inc(wk_full, 1)

            pe.wait_ge(ld_wr, 32)
            for q in range(4):
                project(0, q // 2, q % 2, bank[q % 4])
            kv = slice(RQ, RQ + RKV)
            for i in range(4):
                pe.wait_ge(kvcd, 2 * i + 2)
                pe.wait_ge(qcd, i + 1)
                for t in range(4 * i, 4 * i + 4):
                    mm = pe.matmul(bank[4][:, t:t + 1], kvq[kv, P * t:P * t + P], ones[kv, 0:1],
                                   start=True, stop=True)
            mm.then_inc(msd, 1)
            pe.wait_ge(krd, 2)
            for i in range(4):
                for t in range(4 * i, 4 * i + 4):
                    mm = pe.matmul(bank[4 + i][kv, P * (t % 4):P * (t % 4) + P], krb[:, RKV * t:RKV * t + RKV],
                                   ident[:, :], start=True, stop=True)
                mm.then_inc(rbd, 1)
            pe.wait_ge(wql_ok, 1)
            pe.wait_ge(ld_qc[0], 16 * NC)
            for q in range(4, 8):
                pe.wait_ge(wk_free, q - 3)
                project(0, q // 2, q % 2, bank[q % 4])
            pe.wait_ge(gscaled, 2)

            def content(i):
                c = slice(CH * i, CH * i + CH)
                pe.wait_ge(kvnd, i + 1)
                pe.matmul(con_bank[0][i][:, :], wkd[kv, :], kvn[kv, c], start=True, stop=True).then_inc(cond, 1)
                pe.wait_ge(wk_free, 5 + i)
                pe.matmul(con_bank[1][i][:, :], wqd[:, :], qcf[:, c], start=True, stop=True).then_inc(cond, 1)

            content(0)
            content(1)
            for i in range(4):
                pe.wait_ge(conl, 2 * i + 1 if i < 2 else 2 * (i - 2) + 2)
                for t in range(4):
                    mm = pe.matmul(val_bank[i][:, P * t:P * t + P], kvn[kv, CH * i + P * t:CH * i + P * t + P],
                                   wvd[kv, :], start=True, stop=True)
                mm.then_inc(vpd, 1)
            content(2)
            content(3)

            def max_chunk(u, p, c, j, k):
                n = PER_UNIT * u + before(c, j) + k
                t, half = (k, 0) if c == 0 else (k // 2, k % 2)
                width = CH if c and half == 0 else max(P * (t + 1), 2 * P)
                if k == 0 and c == 0:
                    if j == 0:
                        wait(pe, ld_con[p], 16 * (u - p) + 32)
                    wait(pe, ld_stk[p][j], 48 * (u - p) + 96)
                wait(pe, mx_read, n + 1 - len(MX))
                q0 = CH * c + P * t
                k0 = CH * half
                pe.matmul(MX[(before(c, j) + k) % len(MX)][:, 0:width],
                          qs[p][0:QK, j, q0:q0 + P], ks[p][0:QK, j, k0:k0 + width],
                          start=True, stop=True).then_inc(mx_done, 1)

            def turn_max(u, c, j):
                n = HG * c + j
                wait(pe, mx_read, PER_UNIT * u + before(c, j) + WORK[c])
                wait(pe, mrow_ok, 8 * u + n)
                pe.transpose(MT[0:KT, 0:P], m4[:, j, :], ident[:, :]).then_inc(mt_done, 1)

            def score(u, p, c, j, kt):
                n = PER_UNIT * u + before(c, j) + kt
                d = kt - c * KT
                width = CH if d < 0 else max(DIAG[d], 2 * P)
                if kt == 0:
                    wait(pe, ld_m[j], 32 * u + 16 * (c + 1))
                wait(pe, exp_done, n + 1 - len(ST))
                q0 = CH * c + CH - width
                pe.matmul(ST[(before(c, j) + kt) % len(ST)][:, 0:width], ks[p][0:QK + 1, j, P * kt:P * kt + P],
                          qs[p][0:QK + 1, j, q0:q0 + width], start=True, stop=True).then_inc(st_done, 1)

            def quad(u, c, kt, vals_c):
                d = kt - c * KT
                width = CH if d < 0 else DIAG[d]
                if kt == 0:
                    wait(pe, v1_ok if c else v0_ok, u + 1)
                    wait(pe, pv_read, 2 * u + c)
                wait(pe, exp_done, PER_UNIT * u + before(c, HG - 1) + kt + 1)
                if d >= 0:
                    wait(pe, masked, 2 * HG * KT * u + HG * KT * c + KT * (HG - 1) + d + 1)
                for j in range(HG):
                    mm = pe.matmul(PV[32 * j:32 * j + VW, CH - width:CH], vals_c[:, kt, j, :],
                                   probs[c][:, j, p_off(c, kt):p_off(c, kt) + width],
                                   start=(kt == 0), stop=(kt == WORK[c] - 1))
                mm.then_inc(pv_done, 1)

            def turn_sums(u, n):
                wait(pe, pv_read, 2 * u + n + 1)
                wait(pe, wk_free, 8 * (u + 3) if not isinstance(u, int) or u < UNITS - 2 else 8 * UNITS)
                wait(pe, att_ok, 1 + 2 * u + n)
                for t in range(KT):
                    tr = pe.transpose(WK[:, P * t:P * t + P], oT[:, n, P * t:P * t + P], ident[:, :])
                tr.then_inc(wk_full, 1)

            pe.wait_ge(vsd, NT)
            pe.wait_ge(ks_ones, 1)
            for n in range(LEAD):
                m, k = chunk_of(n)
                max_chunk(0, 0, 0, m, k)
                if n >= KT + 1 and (n - 1) % KT == 0:
                    if n == KT + 1:
                        pe.wait_ge(conl, 5)
                    turn_max(0, 0, n // KT - 1)
            pe.wait_ge(conl, 8)
            pe.wait_ge(ks_ones, 3)
            pe.wait_ge(ld_qc[1], 16 * NC)

            def unit(u, p, g, first, last):
                g1 = g if p == 0 else g + 1
                for s in range(ITEMS):
                    c, j = s // HG, s % HG
                    for k in range(SLOTS):
                        for kt in SCORES[c][k]:
                            score(u, p, c, j, kt)
                        nxt, n, m, turn_nxt = plan(s, k)
                        if not (nxt and last):
                            i, kk = chunk_of(n)
                            max_chunk(u + 1 if nxt else u, 1 - p if nxt else p, i // HG, i % HG, kk)
                        if m is not None and not (turn_nxt and last):
                            turn_max(u + 1 if turn_nxt else u, m // HG, m % HG)
                        q = PRODUCTS.get((s, k))
                        if q is not None and not last:
                            if q == 0:
                                wait(pe, ld_wr, 32 * (g1 + 1))
                                wait(pe, att_ok, 1 + 2 * (u - 1))
                            if q == 4:
                                wait(pe, wql_ok, g1 + 1)
                            wait(pe, wk_free, 8 * (u + 1) + q)
                            project(1 - p, q // 2, q % 2, WK)
                        if k == 2 and s in (4, 5) and not first:
                            turn_sums(u - 1, s - 4)
                        if k in (1, 4) and s < 4 and not first:
                            quad(u - 1, 1, 2 * s + k // 3, vals1)
                        if k == 4 and s >= 4:
                            quad(u, 0, s - 4, vals0)

            unit_loop(pe, unit)
            for kt in range(2 * KT):
                quad(UNITS - 1, 1, kt, vals1)
            for c in range(NC):
                turn_sums(UNITS - 1, c)


def mixture(nc, x, attn, w_o, router, gate_up, down, out):
    wte_d = nc.dram_tensor("wte", (P, P), F32, kind="Internal").ap()
    with ExitStack() as ctx:
        def sb(name, shape, dt=F32):
            return ctx.enter_context(nc.sbuf_tensor(name, shape, dt))

        def sem(name):
            return ctx.enter_context(nc.semaphore(name))

        y1 = sb("y1", [P, NT, D])
        at = sb("at_nat", [P, NT, D])
        attT = sb("attT", [P, B * T])
        xn2 = sb("xn2", [P, NT, D])
        x2T = sb("x2T", [P, B * T])
        xh = sb("xh", [P, B * T], F32R)
        xl = sb("xl", [P, B * T], F32R)
        wo = sb("wo", [P, D])
        rw = sb("rw", [P, E])
        ident2 = sb("ident2", [P, P])
        eps2 = sb("eps2", [P, 1])
        rev = sb("rev", [P, NT, E])
        stats2 = sb("stats2", [P, NT, 6])
        mv2 = sb("mv2", [P, NT, 2])
        rstd2 = sb("rstd2", [P, NT])
        lg, pr, eq, o1, p2, o2, wte = [sb(n, [P, NT, E]) for n in ("lg", "pr", "eq", "o1", "p2", "o2", "wte_s")]
        mx, sm, m1, f1, m2, f2 = [sb(n, [P, NT]) for n in ("mx", "sm", "m1", "f1", "m2", "f2")]
        wteT = sb("wteT", [P, P])
        raw = [sb(f"raw{p}", [P, WC]) for p in range(2)]
        wh = [sb(f"wh{p}", [P, WC], F32R) for p in range(2)]
        wl = [sb(f"wl{p}", [P, WC], F32R) for p in range(2)]
        wb = [sb(f"wb{p}", [P, B * T]) for p in range(2)]
        sg = sb("sg", [P, 2, CH])
        hf = sb("hf", [P, 2, CH])
        hh = sb("hh", [P, 2, len(IT), CH], F32R)
        hl = sb("hl", [P, 2, len(IT), CH], F32R)
        yw = sb("yw", [P, 2, CH])
        acc = sb("acc", [P, B * T])
        bank = [ctx.enter_context(nc.psum_tensor(f"mbank{i}", [P, CH], F32)) for i in range(8)]
        GB, UB, YB = bank[0:2], bank[2:4], bank[4:6]

        ld_at = [sem(f"ld_at{i}") for i in range(NB)]
        ld_y = sem("ld_y")
        ld_wo = sem("ld_wo")
        ld_raw = [sem(f"ld_raw{p}") for p in range(2)]
        ld_wb = [sem(f"ld_wb{p}") for p in range(2)]
        const2 = sem("const2")
        at_turned = sem("at_turned")
        attT_ok = sem("attT_ok")
        wo_done = sem("wo_done")
        y1_ok = sem("y1_ok")
        bn_ok = sem("bn_ok")
        mv_ok = sem("mv_ok")
        sq_ok = sem("sq_ok")
        rs_ok = sem("rs_ok")
        xn2_ok = sem("xn2_ok")
        x_turned = sem("x_turned")
        xh_ok = sem("xh_ok")
        x2T_ok = sem("x2T_ok")
        xl_ok = sem("xl_ok")
        logit_ok = sem("logit_ok")
        route = sem("route")
        exp_ok = sem("exp_ok")
        wte_turned = sem("wte_turned")
        wteT_ok = sem("wteT_ok")
        wte_st = sem("wte_st")
        pad_ok = sem("pad_ok")
        wh_ok = sem("wh_ok")
        wl_ok = sem("wl_ok")
        g_full = sem("g_full")
        u_full = sem("u_full")
        silu_ok = sem("silu_ok")
        hid_ok = sem("hid_ok")
        hh_ok = sem("hh_ok")
        hl_ok = sem("hl_ok")
        y_full = sem("y_full")
        y_read = sem("y_read")
        acc_ok = sem("acc_ok")
        acc_turned = sem("acc_turned")
        out_ok = sem("out_ok")
        out_done = sem("out_done")
        sp_passed = sem("sp_passed2")

        block = ctx.enter_context(nc.Block())

        def wait(eng, s, v):
            if not isinstance(v, int) or v > 0:
                eng.wait_ge(s, v)

        def pair_loop(eng, pair):
            pair(0)
            with eng.Fori(1, E // 2 - 1) as k:
                pair(k)
            pair(E // 2 - 1)

        def is_last(k, p):
            return isinstance(k, int) and k == E // 2 - 1 and p == 1

        @block.sync
        def _(sp):
            for i in range(NB):
                sp.dma_start(at[:, KT * i:KT * i + KT, :], attn[:, KT * i:KT * i + KT, :]).then_inc(ld_at[i], 16)
            sp.dma_start(wo[:, :], w_o).then_inc(ld_wo, 16)
            sp.dma_start(y1[:, :, :], x).then_inc(ld_y, 16)
            sp.dma_start(rw[:, :], router).then_inc(ld_wo, 16)

            def load_weights(k, p):
                wait(sp, wl_ok, 2 * k + p - 1)
                if isinstance(k, int) and k == 0:
                    sp.wait_ge(pad_ok, 2)
                sp.sem_inc(sp_passed, 1)
                e = bass.ds(2 * k + p, 1)
                sp.dma_start(raw[p][:, 0:GU], gate_up[e, :, :]).then_inc(ld_raw[p], 16)
                for r in range(len(IT)):
                    sp.dma_start(raw[p][0:IT[r], GU + D * r:GU + D * r + D],
                                 down[e, P * r:P * r + IT[r], :]).then_inc(ld_raw[p], 16)

            def load_tokens(k, p):
                wait(sp, y_read, 4 * (2 * k + p - 1))
                sp.sem_inc(sp_passed, 1)
                src = wte_d.rearrange("(t e) n -> e t n", e=E)[bass.ds(2 * k + p, 1), :, :]
                sp.dma_start(wb[p][:, :].rearrange("p (t n) -> p t n", n=P),
                             src.to_broadcast([P, NT, P])).then_inc(ld_wb[p], 16)

            for p in range(2):
                load_weights(0, p)
            sp.wait_ge(wteT_ok, 1)
            sp.dma_start(wte_d, wteT[:, :]).then_inc(wte_st, 16)
            sp.wait_ge(wte_st, 16)
            for p in range(2):
                load_tokens(0, p)
            with sp.Fori(1, E // 2) as k:
                for p in range(2):
                    load_weights(k, p)
                    load_tokens(k, p)
            for i in range(NB):
                sp.wait_ge(out_ok, i + 1)
                sp.dma_start(out[:, KT * i:KT * i + KT, :], y1[:, KT * i:KT * i + KT, :]).then_inc(out_done, 16)
            sp.wait_ge(out_done, 16 * NB)

        @block.gpsimd
        def _(pool):
            pool.memset(ident2[:, :], 0.0).then_inc(const2, 1)
            pool.wait_ge(const2, 1)
            pool.affine_select(out=ident2[:, :], in_=ident2[:, :], compare_op=ALU.not_equal, fill=1.0, base=0,
                               pattern=[[-1, P]], channel_multiplier=1).then_inc(const2, 1)
            pool.memset(eps2[:, :], 1e-5).then_inc(const2, 1)
            for e in range(E):
                pool.memset(rev[:, :, e], float(E - e)).then_inc(const2, 1)
            pool.memset(acc[:, :], 0.0).then_inc(const2, 1)

            def low(n):
                k, p = n
                wait(pool, wh_ok, 2 * k + p + 1)
                pool.tensor_tensor(out=wl[p][:, :], in0=raw[p][:, :], in1=wh[p][:, :].bitcast(F32),
                                   op=ALU.subtract).then_inc(wl_ok, 1)

            def add(n, c):
                wait(pool, y_read, n + 1)
                wait(pool, acc_ok, n - NB + 1)
                pool.tensor_tensor(out=acc[:, CH * c:CH * c + CH], in0=acc[:, CH * c:CH * c + CH],
                                   in1=yw[:, c % 2, :], op=ALU.add).then_inc(acc_ok, 1)

            low((0, 0))
            for i in range(NB):
                pool.wait_ge(xh_ok, i + 1)
                c = slice(CH * i, CH * i + CH)
                pool.tensor_tensor(out=xl[:, c], in0=x2T[:, c], in1=xh[:, c].bitcast(F32),
                                   op=ALU.subtract).then_inc(xl_ok, 1)
            pool.wait_ge(const2, E + 4)

            def pair(k):
                for p in range(2):
                    for c in range(NB):
                        n = NB * (2 * k + p) + c
                        if not isinstance(n, int) or n >= 2:
                            add(n - 2, (c - 2) % NB)
                        if c == 1 and not is_last(k, p):
                            low((k, 1) if p == 0 else (k + 1, 0))

            pair_loop(pool, pair)
            for c in (2, 3):
                add(NB * (E - 1) + c, c)

        @block.scalar
        def _(act):
            for i in range(NB):
                act.wait_ge(at_turned, i + 1)
                act.activation(attT[:, CH * i:CH * i + CH], bank[i][:, :], ACT.Copy).then_inc(attT_ok, 1)
            act.wait_ge(const2, E + 4)

            def high_weights(k, p):
                wait(act, ld_raw[p], 64 * (k + 1))
                wait(act, y_full, NB * (2 * k + p - 1))
                act.activation(wh[p][:, :], raw[p][:, :], ACT.Copy).then_inc(wh_ok, 1)

            def root(i):
                act.wait_ge(mv_ok, KT * i + KT)
                act.activation(rstd2[:, KT * i:KT * i + KT], mv2[:, KT * i:KT * i + KT, 1], ACT.Sqrt,
                               bias=eps2[:, 0:1]).then_inc(sq_ok, 1)

            root(0)
            high_weights(0, 0)
            root(1)
            for i in range(NB):
                if i + 2 < NB:
                    root(i + 2)
                c = slice(CH * i, CH * i + CH)
                act.wait_ge(x_turned, i + 1)
                act.activation(x2T[:, c], bank[i][:, :], ACT.Copy).then_inc(x2T_ok, 1)
                act.activation(xh[:, c], bank[i][:, :], ACT.Copy).then_inc(xh_ok, 1)
            act.wait_ge(route, 2)
            act.activation(pr[:, :, :], lg[:, :, :], ACT.Exp).then_inc(exp_ok, 1)

            def silu(m, i, b):
                wait(act, g_full, m + 1)
                wait(act, hid_ok, m - 1)
                act.activation(sg[0:IT[i], b, :], GB[b][0:IT[i], :], ACT.Silu).then_inc(silu_ok, 1)

            def high(m, n, i, b, bn):
                wait(act, hid_ok, m + 1)
                wait(act, y_full, n - 1)
                act.activation(hh[0:IT[i], bn, i, :], hf[0:IT[i], b, :], ACT.Copy).then_inc(hh_ok, 1)

            def pair(k):
                for p in range(2):
                    for c in range(NB):
                        n = NB * (2 * k + p) + c
                        if isinstance(n, int) and n == 1:
                            act.wait_ge(wte_turned, 1)
                            act.activation(wteT[:, :], bank[7][:, 0:P], ACT.Copy).then_inc(wteT_ok, 1)
                        for i in range(3):
                            m = 3 * n + i
                            b = (c + i) % 2
                            silu(m, i, b)
                            if i:
                                high(m - 1, n, i - 1, 1 - b, c % 2)
                            elif not isinstance(n, int) or n > 0:
                                high(m - 1, n - 1, 2, 1 - b, (c - 1) % 2)
                        if c == 1 and not is_last(k, p):
                            high_weights(*((k, 1) if p == 0 else (k + 1, 0)))

            pair_loop(act, pair)
            high(3 * NB * E - 1, NB * E - 1, 2, 1, 1)

        @block.vector
        def _(dve):
            def bc(v):
                return v[:, :].rearrange("p (t o) -> p t o", o=1).to_broadcast([P, NT, E])

            for p in range(2):
                dve.memset(raw[p][IT[2]:P, GU + 2 * D:WC], 0.0).then_inc(pad_ok, 1)
            dve.wait_ge(ld_y, 16)

            def residual(i):
                dve.wait_ge(wo_done, i + 1)
                part = y1[:, KT * i:KT * i + KT, :]
                dve.tensor_tensor(out=part, in0=bank[4 + i][:, :].rearrange("p (t c) -> p t c", c=D), in1=part,
                                  op=ALU.add).then_inc(y1_ok, 1)
                dve.wait_ge(y1_ok, i + 1)
                for t in range(KT * i, KT * i + KT):
                    dve.bn_stats(stats2[:, t, :], y1[:, t, :]).then_inc(bn_ok, 1)
                for t in range(KT * i, KT * i + KT):
                    dve.wait_ge(bn_ok, t + 1)
                    dve.bn_aggr(mv2[:, t, :], stats2[:, t, :]).then_inc(mv_ok, 1)

            residual(0)
            for i in range(NB):
                if i + 1 < NB:
                    residual(i + 1)
                dve.wait_ge(sq_ok, i + 1)
                dve.reciprocal(rstd2[:, KT * i:KT * i + KT], rstd2[:, KT * i:KT * i + KT]).then_inc(rs_ok, 1)
                dve.wait_ge(rs_ok, i + 1)
                for t in range(KT * i, KT * i + KT):
                    dve.tensor_scalar(xn2[:, t, :], y1[:, t, :], mv2[:, t, 0:1], rstd2[:, t:t + 1],
                                      ALU.subtract, ALU.mult).then_inc(xn2_ok, 1)
            dve.wait_ge(logit_ok, 1)
            logits = bank[6][:, 0:NT * E].rearrange("p (t e) -> p t e", e=E)
            X = mybir.AxisListType.X
            done = 0

            def step(ins):
                nonlocal done
                ins.then_inc(route, 1)
                done += 1
                dve.wait_ge(route, done)

            step(dve.tensor_reduce(mx[:, :], logits, X, ALU.max))
            step(dve.tensor_tensor(out=lg[:, :, :], in0=logits, in1=bc(mx), op=ALU.subtract))
            dve.wait_ge(exp_ok, 1)
            step(dve.tensor_reduce(sm[:, :], pr[:, :, :], X, ALU.add))
            step(dve.reciprocal(sm[:, :], sm[:, :]))
            step(dve.tensor_tensor(out=pr[:, :, :], in0=pr[:, :, :], in1=bc(sm), op=ALU.mult))
            for src, m, f, o in ((pr, m1, f1, o1), (p2, m2, f2, o2)):
                step(dve.tensor_reduce(m[:, :], src[:, :, :], X, ALU.max))
                step(dve.tensor_tensor(out=eq[:, :, :], in0=src[:, :, :], in1=bc(m), op=ALU.is_equal))
                step(dve.tensor_tensor(out=eq[:, :, :], in0=eq[:, :, :], in1=rev[:, :, :], op=ALU.mult))
                step(dve.tensor_reduce(f[:, :], eq[:, :, :], X, ALU.max))
                step(dve.tensor_tensor(out=o[:, :, :], in0=eq[:, :, :], in1=bc(f), op=ALU.is_equal))
                if o is o1:
                    step(dve.scalar_tensor_tensor(out=p2[:, :, :], in0=o1[:, :, :], scalar=-2.0, in1=pr[:, :, :],
                                                  op0=ALU.mult, op1=ALU.add))
            step(dve.tensor_tensor(out=o2[:, :, :], in0=o2[:, :, :], in1=o1[:, :, :], op=ALU.add))
            step(dve.tensor_tensor(out=wte[:, :, :], in0=pr[:, :, :], in1=o2[:, :, :], op=ALU.mult))

            def hidden(m, i, b):
                wait(dve, u_full, m + 1)
                wait(dve, silu_ok, m + 1)
                wait(dve, hl_ok, m - 1)
                dve.tensor_tensor(out=hf[0:IT[i], b, :], in0=UB[b][0:IT[i], :], in1=sg[0:IT[i], b, :],
                                  op=ALU.mult).then_inc(hid_ok, 1)

            def low(m, i, b, bn):
                wait(dve, hh_ok, m + 1)
                dve.tensor_tensor(out=hl[0:IT[i], bn, i, :], in0=hf[0:IT[i], b, :],
                                  in1=hh[0:IT[i], bn, i, :].bitcast(F32), op=ALU.subtract).then_inc(hl_ok, 1)

            def weigh(n, c, p, k):
                wait(dve, y_full, n + 1)
                wait(dve, ld_wb[p], 16 * (k + 1))
                wait(dve, acc_ok, n - 1)
                dve.tensor_tensor(out=yw[:, c % 2, :], in0=YB[c % 2][:, :], in1=wb[p][:, CH * c:CH * c + CH],
                                  op=ALU.mult).then_inc(y_read, 1)

            def pair(k):
                for p in range(2):
                    for c in range(NB):
                        n = NB * (2 * k + p) + c
                        for i in range(3):
                            m = 3 * n + i
                            b = (c + i) % 2
                            hidden(m, i, b)
                            if i:
                                low(m - 1, i - 1, 1 - b, c % 2)
                            elif not isinstance(n, int) or n > 0:
                                low(m - 1, 2, 1 - b, (c - 1) % 2)
                            if i == 0 and (not isinstance(n, int) or n > 1):
                                if c >= 2:
                                    weigh(n - 2, c - 2, p, k)
                                else:
                                    weigh(n - 2, c + 2, 1 - p, k if p else k - 1)

            pair_loop(dve, pair)
            low(3 * NB * E - 1, 2, 1, 1)
            for c in (2, 3):
                weigh(NB * (E - 1) + c, c, 1, E // 2 - 1)
            for i in range(NB):
                dve.wait_ge(acc_turned, i + 1)
                part = y1[:, KT * i:KT * i + KT, :]
                dve.tensor_tensor(out=part, in0=bank[i][:, :].rearrange("p (t c) -> p t c", c=D), in1=part,
                                  op=ALU.add).then_inc(out_ok, 1)

        @block.tensor
        def _(pe):
            pe.wait_ge(const2, 3)
            for i in range(NB):
                pe.wait_ge(ld_at[i], 16)
                for t in range(KT):
                    tr = pe.transpose(bank[i][:, P * t:P * t + P], at[:, KT * i + t, :], ident2[:, :])
                tr.then_inc(at_turned, 1)
            pe.wait_ge(ld_wo, 32)

            def turn_x(i):
                for t in range(KT):
                    pe.wait_ge(xn2_ok, KT * i + t + 1)
                    tr = pe.transpose(bank[i][:, P * t:P * t + P], xn2[:, KT * i + t, :], ident2[:, :])
                tr.then_inc(x_turned, 1)

            for i in range(NB):
                pe.wait_ge(attT_ok, i + 1)
                for t in range(KT):
                    q = CH * i + P * t
                    mm = pe.matmul(bank[4 + i][:, P * t:P * t + P], attT[:, q:q + P], wo[:, :], start=True, stop=True)
                mm.then_inc(wo_done, 1)

            def logits(i):
                pe.wait_ge(x2T_ok, i + 1)
                for t in range(KT * i, KT * i + KT):
                    mm = pe.matmul(bank[6][:, E * t:E * t + E], x2T[:, P * t:P * t + P], rw[:, :],
                                   start=True, stop=True)
                return mm

            turn_x(0)
            pe.wait_ge(y1_ok, 3)
            for i in range(1, NB):
                turn_x(i)
                logits(i - 1)
            logits(NB - 1).then_inc(logit_ok, 1)
            pe.wait_ge(y1_ok, NB)
            pe.wait_ge(xh_ok, NB)

            def split3(dst, w, v, k, start, stop):
                (w_h, w_l), (v_h, v_l) = w, v
                pe.matmul(dst, w_h, v_h, start=start, stop=False)
                pe.matmul(dst, w_h, v_l, start=False, stop=False)
                return pe.matmul(dst, w_l, v_h, start=False, stop=stop)

            def project(m, p, c, i, b):
                v = [s[:, CH * c:CH * c + CH] for s in (xh, xl)]
                wait(pe, silu_ok, m - 1)
                cols = slice(P * i, P * i + IT[i])
                split3(GB[b][0:IT[i], :], [w[p][:, cols] for w in (wh, wl)], v, P, True, True).then_inc(g_full, 1)
                wait(pe, hid_ok, m - 1)
                cols = slice(I + P * i, I + P * i + IT[i])
                split3(UB[b][0:IT[i], :], [w[p][:, cols] for w in (wh, wl)], v, P, True, True).then_inc(u_full, 1)

            def down_product(n, p, c, i):
                wait(pe, hl_ok, 3 * n + i + 1)
                if i == 0:
                    wait(pe, y_read, n - 1)
                r = slice(0, IT[i])
                cols = slice(GU + D * i, GU + D * i + D)
                mm = split3(YB[c % 2][:, :], [w[p][r, cols] for w in (wh, wl)],
                            [s[r, c % 2, i, :] for s in (hh, hl)], IT[i], i == 0, i == 2)
                if i == 2:
                    mm.then_inc(y_full, 1)

            def turn_wte():
                pe.wait_ge(route, 18)
                pe.transpose(bank[7][:, 0:P], wte[:, :, :].rearrange("p t e -> p (t e)"), ident2[:, :])\
                  .then_inc(wte_turned, 1)

            def pair(k):
                for p in range(2):
                    for c in range(NB):
                        n = NB * (2 * k + p) + c
                        if c == 0:
                            wait(pe, wl_ok, 2 * k + p + 1)
                        if isinstance(n, int) and n < NB:
                            pe.wait_ge(xl_ok, n + 1)
                        for i in range(3):
                            project(3 * n + i, p, c, i, (c + i) % 2)
                            if isinstance(n, int) and 3 * n + i == 1:
                                turn_wte()
                            if not isinstance(n, int) or n > 0:
                                down_product(n - 1, p if c else 1 - p, (c - 1) % NB, i)

            pair_loop(pe, pair)
            for i in range(3):
                down_product(NB * E - 1, 1, NB - 1, i)
            for i in range(NB):
                pe.wait_ge(acc_ok, NB * (E - 1) + i + 1)
                if i == 0:
                    pe.wait_ge(hid_ok, 3 * NB * E)
                for t in range(KT):
                    q = CH * i + P * t
                    tr = pe.transpose(bank[i][:, P * t:P * t + P], acc[:, q:q + P], ident2[:, :])
                tr.then_inc(acc_turned, 1)


def block_kernel(nc, x, w_qkv, w_kdec, w_vdec, w_qdec, g_kv, w_kr, w_qr, cosT, sinT, w_o, router, gate_up, down, out):
    attn = nc.dram_tensor("attn", (P, NT, H * DH), F32, kind="Internal").ap()
    attention(nc, x, w_qkv, w_kdec, w_vdec, w_qdec, g_kv, w_kr, w_qr, cosT, sinT, attn)
    mixture(nc, x, attn, w_o, router, gate_up, down, out)


def tables():
    inv_freq = 1.0 / 10000.0 ** (np.arange(0, R, 2, dtype=np.float32) / R)
    freqs = np.outer(np.arange(T, dtype=np.float32), inv_freq)
    emb = np.concatenate([freqs, freqs], -1).T
    sign = np.where(np.arange(R) < R // 2, -1.0, 1.0).astype(np.float32)[:, None]
    return np.tile(np.cos(emb), (HG, 1)), np.tile(np.sin(emb) * sign, (HG, 1))


def by_feature(w):
    return w.reshape(-1, H, DH).transpose(0, 2, 1).reshape(w.shape)


def partners(w):
    halves = w.reshape(w.shape[0], H, 2, R // 2)
    return np.stack([w, halves[:, :, ::-1].reshape(w.shape)], 1)


def kernel(**inputs):
    import concourse.bacc as bacc
    from concourse.bass_utils import run_bass_kernel_spmd

    a = {k: np.asarray(v) for k, v in inputs.items()}
    at, ff = "L0_attn_", "L0_ffn_"
    cos, sin = tables()
    ins = dict(
        x=a[at + "x"].reshape(NT, P, D).transpose(1, 0, 2),
        w_qkv=np.concatenate([a[at + "W_q"], a[at + "W_kv"]], 1),
        w_kdec=by_feature(a[at + "W_kdec"]), w_vdec=a[at + "W_vdec"], w_qdec=by_feature(a[at + "W_qdec"]),
        g_kv=a[at + "g_kv"][:, None],
        w_kr=partners(a[at + "W_krope"]), w_qr=np.concatenate([partners(a[at + "W_qrope"])] * 2, 0),
        cosT=cos, sinT=sin,
        w_o=a[at + "W_o"],
        router=a[ff + "router_w"].T,
        gate_up=np.concatenate([a[ff + "gate_w"].transpose(0, 2, 1), a[ff + "up_w"].transpose(0, 2, 1)], 2),
        down=a[ff + "down_w"].transpose(0, 2, 1),
    )
    ins = {k: np.ascontiguousarray(v) for k, v in ins.items()}
    nc = bacc.Bacc("TRN2", target_bir_lowering=False, num_devices=1)
    args = [nc.dram_tensor(k, v.shape, mybir.dt.from_np(v.dtype), kind="ExternalInput").ap() for k, v in ins.items()]
    out = nc.dram_tensor("out", (P, NT, D), F32, kind="ExternalOutput").ap()
    block_kernel(nc, *args, out)
    r = run_bass_kernel_spmd(nc, [ins], core_ids=[0])
    return np.asarray(r.results[0]["out"]).transpose(1, 0, 2).reshape(B, T, D)
```
